# Optimizing a Trainium2 kernel written in Bass

```python
import numpy as np
import jax
import jax.numpy as jnp

def _softmax(x, axis=-1):
    return jax.nn.softmax(x, axis=axis)

def _gelu(x):
    return jax.nn.gelu(x, approximate=True)

def _silu(x):
    return jax.nn.silu(x)

def _sigmoid(x):
    return jax.nn.sigmoid(x)

def _layernorm(x, axis=-1, eps=1e-05):
    m = jnp.mean(x, axis=axis, keepdims=True)
    v = jnp.var(x, axis=axis, keepdims=True)
    return (x - m) / jnp.sqrt(v + eps)

def _scatter_add(tgt, idx, src, axis=0):
    return tgt.at[idx].add(src)

def _segment_sum(src, seg, n):
    return jax.ops.segment_sum(src, seg, n)
kernel_name = 'mk_adj_seq_d2_adj_r2_145a86'

def setup_inputs(seed: int=0):
    np.random.seed(seed)
    _w = jnp.asarray

    def _rec_inputs():
        import jax
        import jax.numpy as jnp
        _gk = jax.random.key(seed)
        x = -0.0005207 + 1.001 * jax.random.normal(jax.random.fold_in(_gk, 1), (128, 64, 256), jnp.float32)
        _a = jax.random.bernoulli(jax.random.fold_in(_gk, 2), 0.125, (128, 64, 64))
        _a = jnp.logical_or(_a, jnp.eye(64, dtype=bool))
        adj = _a.astype(jnp.int32)
        return (x, adj)
    x, adj = _rec_inputs()

    def _L0_gnn_setup():
        import jax, jax.numpy as jnp
        import numpy as np
        B, S, D, H = (2, 1024, 256, 8)
        HD = D // H
        EPS = 1e-05

        def _ln(x, g, b):
            mu = jnp.mean(x, axis=-1, keepdims=True)
            var = jnp.mean((x - mu) ** 2, axis=-1, keepdims=True)
            return (x - mu) * jax.lax.rsqrt(var + EPS) * g + b
        key = jax.random.key(seed)
        ks = jax.random.split(key, 16)
        x = jax.random.normal(ks[0], (B, S, D), dtype=jnp.float32)
        adj = jax.random.randint(ks[1], (B, S, S), 0, 2, dtype=jnp.int32)
        adj = adj.at[:, jnp.arange(S), jnp.arange(S)].set(1)
        edge_attr = jax.random.normal(ks[2], (B, S, S), dtype=jnp.float32)
        sc = 1.0 / np.sqrt(D)
        p = lambda k, shp: jax.random.normal(k, shp, dtype=jnp.float32) * sc
        return {'x': x, 'adj_matrix': adj, 'edge_attr_matrix': edge_attr, 'ln1_g': jnp.ones((D,)), 'ln1_b': jnp.zeros((D,)), 'ln2_g': jnp.ones((D,)), 'ln2_b': jnp.zeros((D,)), 'wq': p(ks[3], (D, D)), 'bq': jnp.zeros((D,)), 'wk': p(ks[4], (D, D)), 'bk': jnp.zeros((D,)), 'wv': p(ks[5], (D, D)), 'bv': jnp.zeros((D,)), 'wo': p(ks[6], (D, D)), 'bo': jnp.zeros((D,)), 'w1': p(ks[7], (D, 4 * D)), 'b1': jnp.zeros((4 * D,)), 'w2': p(ks[8], (4 * D, D)), 'b2': jnp.zeros((D,))}
    _L0_gnn_all = _L0_gnn_setup()
    _L0_gnn_in = {k: v for k, v in _L0_gnn_all.items() if k in ('ln1_g', 'ln1_b', 'ln2_g', 'ln2_b', 'wq', 'bq', 'wk', 'bk', 'wv', 'bv', 'wo', 'bo', 'w1', 'b1', 'w2', 'b2')}
    del _L0_gnn_all

    def _L1_gnn_setup():
        import jax, jax.numpy as jnp
        import numpy as np
        B, N, E, FF, L = (8, 1024, 256, 128, 2)
        LN_EPS = 1e-05
        SCALE = float(np.sqrt(FF))

        def layer_norm(x, g, b):
            m = jnp.mean(x, axis=-1, keepdims=True)
            v = jnp.mean(jnp.square(x - m), axis=-1, keepdims=True)
            return (x - m) * jax.lax.rsqrt(v + LN_EPS) * g + b
        key = jax.random.key(seed)
        ks = jax.random.split(key, 9)
        s = 0.02
        node_fts = jax.random.normal(ks[0], (B, N, E), jnp.float32)
        rel_edges = jax.random.randint(ks[1], (B, N, N), 0, 2, jnp.int32)
        Wq = jax.random.normal(ks[2], (L, FF, E), jnp.float32) * s
        bq = jnp.zeros((L, FF), jnp.float32)
        Wk = jax.random.normal(ks[3], (L, FF, E), jnp.float32) * s
        bk = jnp.zeros((L, FF), jnp.float32)
        Wc = jax.random.normal(ks[4], (L, E, E), jnp.float32) * s
        ln_g = jnp.ones((L, E), jnp.float32)
        ln_b = jnp.zeros((L, E), jnp.float32)
        return {'node_fts': node_fts, 'rel_edges': rel_edges, 'Wq': Wq, 'bq': bq, 'Wk': Wk, 'bk': bk, 'Wc': Wc, 'ln_g': ln_g, 'ln_b': ln_b}
    _L1_gnn_all = _L1_gnn_setup()
    _L1_gnn_in = {k: v for k, v in _L1_gnn_all.items() if k in ('Wq', 'bq', 'Wk', 'bk', 'Wc', 'ln_g', 'ln_b')}
    del _L1_gnn_all
    return {'x': x, 'adj': adj, 'L0_gnn_ln1_g': _L0_gnn_in['ln1_g'], 'L0_gnn_ln1_b': _L0_gnn_in['ln1_b'], 'L0_gnn_ln2_g': _L0_gnn_in['ln2_g'], 'L0_gnn_ln2_b': _L0_gnn_in['ln2_b'], 'L0_gnn_wq': _L0_gnn_in['wq'], 'L0_gnn_bq': _L0_gnn_in['bq'], 'L0_gnn_wk': _L0_gnn_in['wk'], 'L0_gnn_bk': _L0_gnn_in['bk'], 'L0_gnn_wv': _L0_gnn_in['wv'], 'L0_gnn_bv': _L0_gnn_in['bv'], 'L0_gnn_wo': _L0_gnn_in['wo'], 'L0_gnn_bo': _L0_gnn_in['bo'], 'L0_gnn_w1': _L0_gnn_in['w1'], 'L0_gnn_b1': _L0_gnn_in['b1'], 'L0_gnn_w2': _L0_gnn_in['w2'], 'L0_gnn_b2': _L0_gnn_in['b2'], 'L1_gnn_Wq': _L1_gnn_in['Wq'], 'L1_gnn_bq': _L1_gnn_in['bq'], 'L1_gnn_Wk': _L1_gnn_in['Wk'], 'L1_gnn_bk': _L1_gnn_in['bk'], 'L1_gnn_Wc': _L1_gnn_in['Wc'], 'L1_gnn_ln_g': _L1_gnn_in['ln_g'], 'L1_gnn_ln_b': _L1_gnn_in['ln_b']}

def reference(x, adj, L0_gnn_ln1_g, L0_gnn_ln1_b, L0_gnn_ln2_g, L0_gnn_ln2_b, L0_gnn_wq, L0_gnn_bq, L0_gnn_wk, L0_gnn_bk, L0_gnn_wv, L0_gnn_bv, L0_gnn_wo, L0_gnn_bo, L0_gnn_w1, L0_gnn_b1, L0_gnn_w2, L0_gnn_b2, L1_gnn_Wq, L1_gnn_bq, L1_gnn_Wk, L1_gnn_bk, L1_gnn_Wc, L1_gnn_ln_g, L1_gnn_ln_b):
    import jax
    import jax.numpy as jnp

    def _L0_gnn_ref(x, adj_matrix, edge_attr_matrix, ln1_g, ln1_b, ln2_g, ln2_b, wq, bq, wk, bk, wv, bv, wo, bo, w1, b1, w2, b2):
        import jax, jax.numpy as jnp
        import numpy as np
        B, S, D, H = (2, 1024, 256, 8)
        HD = D // H
        EPS = 1e-05

        def _ln(x, g, b):
            mu = jnp.mean(x, axis=-1, keepdims=True)
            var = jnp.mean((x - mu) ** 2, axis=-1, keepdims=True)
            return (x - mu) * jax.lax.rsqrt(var + EPS) * g + b
        b, s, d = x.shape
        residual = x
        nx = _ln(x, ln1_g, ln1_b)
        q = (nx @ wq + bq).reshape(b, s, H, HD).transpose(0, 2, 1, 3)
        k = (nx @ wk + bk).reshape(b, s, H, HD).transpose(0, 2, 1, 3)
        v = (nx @ wv + bv).reshape(b, s, H, HD).transpose(0, 2, 1, 3)
        adjf = adj_matrix.astype(jnp.float32)
        bias = jnp.where(adj_matrix > 0, 0.1 * edge_attr_matrix * adjf, -jnp.inf)[:, None]
        scores = jnp.einsum('bhqd,bhkd->bhqk', q, k) / np.sqrt(HD) + bias
        attn = jax.nn.softmax(scores, axis=-1)
        out = jnp.einsum('bhqk,bhkd->bhqd', attn, v)
        out = out.transpose(0, 2, 1, 3).reshape(b, s, d)
        x1 = residual + (out @ wo + bo)
        n2 = _ln(x1, ln2_g, ln2_b)
        mlp = jax.nn.gelu(n2 @ w1 + b1, approximate=False) @ w2 + b2
        return x1 + mlp

    def _L1_gnn_ref(node_fts, rel_edges, Wq, bq, Wk, bk, Wc, ln_g, ln_b):
        import jax, jax.numpy as jnp
        import numpy as np
        B, N, E, FF, L = (8, 1024, 256, 128, 2)
        LN_EPS = 1e-05
        SCALE = float(np.sqrt(FF))

        def layer_norm(x, g, b):
            m = jnp.mean(x, axis=-1, keepdims=True)
            v = jnp.mean(jnp.square(x - m), axis=-1, keepdims=True)
            return (x - m) * jax.lax.rsqrt(v + LN_EPS) * g + b
        x = node_fts
        mask = rel_edges == 0
        for k in range(L):
            q = jnp.einsum('bnd,fd->bnf', x, Wq[k]) + bq[k]
            kk = jnp.einsum('bnd,fd->bnf', x, Wk[k]) + bk[k]
            scores = jnp.einsum('bof,bif->boi', q, kk) / SCALE
            scores = jnp.where(mask, -10000000000.0, scores)
            attn = jax.nn.softmax(scores, axis=2)
            attn = jnp.where(mask, 0.0, attn)
            ctx = jnp.einsum('boi,bid->bod', attn, x)
            ctx = jnp.einsum('bnd,ed->bne', ctx, Wc[k])
            x = layer_norm(x + ctx, ln_g[k], ln_b[k])
        return x
    x = _L0_gnn_ref(x, adj, adj, L0_gnn_ln1_g, L0_gnn_ln1_b, L0_gnn_ln2_g, L0_gnn_ln2_b, L0_gnn_wq, L0_gnn_bq, L0_gnn_wk, L0_gnn_bk, L0_gnn_wv, L0_gnn_bv, L0_gnn_wo, L0_gnn_bo, L0_gnn_w1, L0_gnn_b1, L0_gnn_w2, L0_gnn_b2)
    x = _L1_gnn_ref(x, adj, L1_gnn_Wq, L1_gnn_bq, L1_gnn_Wk, L1_gnn_bk, L1_gnn_Wc, L1_gnn_ln_g, L1_gnn_ln_b)
    return x

_drawn_inputs = setup_inputs


def setup_inputs(seed=0):
    import zlib

    import numpy as np

    out = dict(_drawn_inputs(seed))
    spreads = {'L0_gnn_ln1_g': (1.0, 0.2),
     'L0_gnn_ln1_b': (0.0, 0.1),
     'L0_gnn_ln2_g': (1.0, 0.2),
     'L0_gnn_ln2_b': (0.0, 0.1),
     'L0_gnn_bq': (0.0, 0.1),
     'L0_gnn_bk': (0.0, 0.8),
     'L0_gnn_bv': (0.0, 0.1),
     'L0_gnn_bo': (0.0, 0.1),
     'L0_gnn_b1': (0.0, 0.1),
     'L0_gnn_b2': (0.0, 0.1),
     'L1_gnn_bq': (0.0, 0.8),
     'L1_gnn_bk': (0.0, 0.8),
     'L1_gnn_ln_g': (1.0, 0.2),
     'L1_gnn_ln_b': (0.0, 0.1)}
    factors = {}
    for name, (base, spread) in spreads.items():
        noise = np.random.default_rng([zlib.crc32(name.encode()), seed]).standard_normal(out[name].shape)
        drawn = base * np.exp(spread * noise) if base else spread * noise
        out[name] = jnp.asarray(drawn.astype(out[name].dtype))
    for name, factor in factors.items():
        out[name] = (out[name] * factor).astype(out[name].dtype)
    return out
```

```python
from contextlib import ExitStack

import concourse.bass as bass
from concourse import mybir

P = 128
TILES = 4
ROWS = TILES * P
NODES = 64
GRAPHS = ROWS // NODES
EPS = 1e-5
MASKED = -1e30

ALU = mybir.AluOpType
ACT = mybir.ActivationFunctionType
F32 = mybir.dt.float32
F32R = mybir.dt.float32r
I32 = mybir.dt.int32
AX_X = mybir.AxisListType.X


def number(jobs):
    first, n = {}, 0
    for name, count in jobs:
        first[name] = n
        n += count
    return first, n


A_JOBS, A_COUNT = number([("xT", 2), ("q", 2), ("k", 2), ("v", 2), ("s", 4), ("p01", 2), ("o01", 1),
                          ("p23", 2), ("o23", 1), ("w", 2)])
M_JOBS, M_COUNT = number([("xT", 2), ("h", 8), ("y", 2)])
L_JOBS, L_COUNT = number([(f"{name}{layer}", count) for layer in range(2)
                          for name, count in (("xT", 2), ("qk", 2), ("xw", 2), ("s", 1), ("p", 1), ("o", 2))])
RING = {"A": 4, "M": 2, "L": 2}
COUNT = {"A": A_COUNT, "M": M_COUNT, "L": L_COUNT}
BASE = {"A": 0, "M": 4, "L": 6}
assert all(COUNT[s] % RING[s] == 0 for s in RING)
P_JOB = [A_JOBS["p01"], A_JOBS["p01"] + 1, A_JOBS["p23"], A_JOBS["p23"] + 1]
O_JOB = [A_JOBS["o01"], A_JOBS["o23"]]


def gnn_kernel(nc, x, adj, ln1_g, ln1_b, ln2_g, ln2_b, wq, bq, wk, bk, wv, bv, wo, bo, w1, b1, w2, b2,
               Wq, bq1, Wk, bk1, Wc, ln_g, ln_b, out):
    B, S, D = x.shape
    F = w1.shape[1]
    FF = Wq.shape[1]
    DC = D // P
    FC = F // P
    H = 8
    HD = D // H
    QUADS = P // HD
    GROUPS = B * S // ROWS
    LAYERS = Wq.shape[0]
    assert S == NODES and D == 256 and HD == 32 and FF == P and LAYERS == 2 and H * NODES == 512
    SCALE0 = float(HD) ** -0.5
    SCALE1 = float(FF) ** -0.5

    x_v = x.rearrange("(G t b) s d -> G (b s) t d", t=TILES, b=2)
    adj_v = adj.rearrange("(G t b) s k -> G (b s) t k", t=TILES, b=2)
    out_v = out.rearrange("(G t b) s d -> G (b s) t d", t=TILES, b=2)

    with ExitStack() as ctx:
        def sb(name, shape, dt=F32):
            return ctx.enter_context(nc.sbuf_tensor(name, shape, dt))

        def sem(name):
            return ctx.enter_context(nc.semaphore(name))

        def split(name, shape):
            return sb(name + "_hi", shape, F32R), sb(name + "_lo", shape, F32R)

        bank = [ctx.enter_context(nc.psum_tensor(f"bank{n}", [P, 512], F32)) for n in range(8)]
        filled = [sem(f"filled{n}") for n in range(8)]
        drained = [sem(f"drained{n}") for n in range(8)]

        w_qkv = split("w_qkv", [P, 3, DC, D])
        w_o = split("w_o", [P, DC, D])
        w_1 = split("w_1", [P, DC, F])
        w_2 = split("w_2", [P, FC, D])
        w_l = split("w_l", [P, LAYERS, 2, DC, FF])
        w_c = split("w_c", [P, LAYERS, DC, D])
        ident = sb("ident", [P, P])
        cols = sb("cols", [P, 40])
        g1c, b1c, g2c, b2c = (cols[:, 2 * n:2 * n + 2] for n in range(4))
        bq_c, bk_c, bv_c = (cols[:, 8 + 2 * n:10 + 2 * n] for n in range(3))
        bh_c = cols[:, 14:22]
        lq_c, lk_c = cols[:, 22:24], cols[:, 24:26]
        bo_row = sb("bo_row", [P, D])
        b2_row = sb("b2_row", [P, D])
        lg_row = sb("lg_row", [P, LAYERS, D])
        lb_row = sb("lb_row", [P, LAYERS, D])
        spare_d, spare_p = cols[:, 26:27], cols[:, 27:28]
        minus_half = cols[:, 28:32]

        x_in = sb("x_in", [P, TILES, D])
        adj_a = sb("adj_a", [P, TILES, NODES], I32)
        pen = sb("pen", [P, TILES, NODES])
        bias0 = sb("bias0", [P, TILES, NODES])
        x_hat = sb("x_hat", [P, TILES, D])
        xT = split("xT", [P, DC, ROWS])
        qT = sb("qT", [P, DC, ROWS])
        kT = sb("kT", [P, DC, GRAPHS, QUADS, NODES])
        v2 = sb("v2", [P, GRAPHS, H // 2, 2, HD])
        top = sb("top", [P, TILES, H])
        total = sb("total", [P, TILES, H])
        share = sb("share", [P, TILES, H])
        sc = sb("sc", [P, TILES, 512])
        pT = qT
        oT = xT
        x1 = sb("x1", [P, TILES, D])
        x1_hat = x_hat
        x1_b2 = sb("x1_b2", [P, TILES, D])
        nT = split("nT", [P, DC, ROWS])
        HB = 2
        hf = sb("hf", [P, HB, ROWS])
        hT = split("hT", [P, FC, ROWS])
        x2 = sb("x2", [P, TILES, D])
        adj_l = sb("adj_l", [P, TILES, NODES], I32)
        pen1 = sb("pen1", [P, TILES, 2, NODES])
        lT = split("lT", [P, DC, ROWS])
        lqk = sb("lqk", [P, 2, ROWS])
        lxw = sb("lxw", [P, TILES, D])
        ls = sb("ls", [P, TILES, P])
        lpT = lqk[:, 0, :].rearrange("p (t n) -> p t n", t=TILES)
        ltop = sb("ltop", [P, TILES])
        lsum = sb("lsum", [P, TILES])
        lshare = sb("lshare", [P, TILES])
        x3 = sb("x3", [P, TILES, D])
        stats = {s: (sb(f"st_{s}", [P, TILES, 6]), sb(f"mv_{s}", [P, TILES, 2]), sb(f"nm_{s}", [P, TILES]),
                     sb(f"ve_{s}", [P, TILES]), sb(f"rs_{s}", [P, TILES])) for s in "AHL"}

        params_loaded = sem("params_loaded")
        raw_loaded = [sem(f"raw_loaded{n}") for n in range(5)]
        consts = sem("consts")
        prep_d = sem("prep_d")
        prep_p = sem("prep_p")
        prep_a = sem("prep_a")
        prep_g = sem("prep_g")
        x_loaded = sem("x_loaded")
        x_used = sem("x_used")
        adj_a_loaded = sem("adj_a_loaded")
        adj_a_used = sem("adj_a_used")
        adj_l_loaded = sem("adj_l_loaded")
        adj_l_used = sem("adj_l_used")
        stored = sem("stored")
        dve_n, dve_a, dve_h, dve_l = sem("dve_n"), sem("dve_a"), sem("dve_h"), sem("dve_l")
        pool_a, pool_h = sem("pool_a"), sem("pool_h")
        stats_a, stats_h, stats_l = sem("stats_a"), sem("stats_h"), sem("stats_l")
        rstd_l = sem("rstd_l")
        x_hat_ready, x1_hat_ready = sem("x_hat_ready"), sem("x1_hat_ready")
        x1_begun, x1_b2_ready = sem("x1_begun"), sem("x1_b2_ready")
        hi_a, hi_m, hi_l = sem("hi_a"), sem("hi_m"), sem("hi_l")
        shifted, exp_done, p_ready = sem("shifted"), sem("exp_done"), sem("p_ready")
        h_lo = sem("h_lo")
        l_top, l_exp, l_x, l_out = sem("l_top"), sem("l_exp"), sem("l_x"), sem("l_out")

        def wait(eng, s, value):
            if not isinstance(value, int) or value > 0:
                eng.wait_ge(s, value)

        def wait_filled(eng, ring, g, job):
            n = BASE[ring] + job % RING[ring]
            wait(eng, filled[n], g * (COUNT[ring] // RING[ring]) + job // RING[ring] + 1)
            return bank[n]

        def wait_drained(eng, ring, g, job):
            wait(eng, drained[BASE[ring] + job % RING[ring]], g * (COUNT[ring] // RING[ring]) + job // RING[ring] + 1)

        def wait_sources(eng, ring, g, sources, job):
            uses = {job % RING[ring]: job // RING[ring]}
            for n in sources:
                uses[n % RING[ring]] = max(uses.get(n % RING[ring], 0), n // RING[ring] + 1)
            for n, count in uses.items():
                wait(eng, drained[BASE[ring] + n], g * (COUNT[ring] // RING[ring]) + count)
            return bank[BASE[ring] + job % RING[ring]]

        def wait_all_drained_before(eng, ring, g, job):
            wait(eng, drained[BASE[ring] + job % RING[ring]], g * (COUNT[ring] // RING[ring])
                 - (COUNT[ring] - 1 - job) // RING[ring])

        def wait_empty(eng, ring, g, job):
            n = BASE[ring] + job % RING[ring]
            wait(eng, drained[n], g * (COUNT[ring] // RING[ring]) + job // RING[ring])
            return bank[n]

        def is_filled(ring, job):
            return filled[BASE[ring] + job % RING[ring]]

        def is_drained(ring, job):
            return drained[BASE[ring] + job % RING[ring]]

        def stages(i):
            return dict(A=i < GROUPS, H=1 <= i <= GROUPS, L=2 <= i <= GROUPS + 1, T=i >= 3, N=i + 1 < GROUPS)

        def run(eng, body):
            for i in range(3):
                body(i, **stages(i))
            with eng.Fori(3, GROUPS - 1) as i:
                body(i, A=True, H=True, L=True, T=True, N=True)
            for i in range(GROUPS - 1, GROUPS + 3):
                body(i, **stages(i))

        raw_qkvo = sc[:, :, :].rearrange("p t n -> p (t n)").rearrange("p (w c n) -> p w c n", w=4, c=DC)
        raw_1 = kT[:, 0].rearrange("p g j k -> p (g j k)").rearrange("p (c n) -> p c n", c=DC)
        raw_2 = kT[:, 1].rearrange("p g j k -> p (g j k)").rearrange("p (f n) -> p f n", f=FC)
        raw_l = v2[:, :, :, :, :].rearrange("p g j a d -> p (g j a d)").rearrange("p (l w e) -> p l w e", l=LAYERS, w=4)

        PARAMS = 26
        param_rows = ls[0:PARAMS, 0, :]

        block = ctx.enter_context(nc.Block())

        @block.sync
        def _(sp):
            row = lambda v: v.rearrange("(a n) -> a n", a=1).to_broadcast([P, v.shape[0]])
            for n, w in enumerate((wq, wk, wv, wo)):
                sp.dma_start(raw_qkvo[:, n], w.rearrange("(c p) n -> p c n", p=P)).then_inc(raw_loaded[0], 16)
            sp.dma_start(x_in[:], x_v[0]).then_inc(x_loaded, 16)
            sp.dma_start(adj_a[:], adj_v[0]).then_inc(adj_a_loaded, 16)
            at = 0
            for v in (ln1_g, ln1_b, ln2_g, ln2_b, bq, bk, bv, b1):
                n = v.shape[0] // P
                sp.dma_start(param_rows[at:at + n, :], v.rearrange("(c p) -> c p", p=P)).then_inc(params_loaded, 16)
                at += n
            for v in (bq1, bk1):
                sp.dma_start(param_rows[at:at + LAYERS, :], v).then_inc(params_loaded, 16)
                at += LAYERS
            assert at == PARAMS
            sp.dma_start(bo_row[:], row(bo)).then_inc(params_loaded, 16)
            sp.dma_start(b2_row[:], row(b2)).then_inc(params_loaded, 16)
            for n in range(LAYERS):
                sp.dma_start(lg_row[:, n], row(ln_g[n])).then_inc(params_loaded, 16)
                sp.dma_start(lb_row[:, n], row(ln_b[n])).then_inc(params_loaded, 16)
            sp.dma_start(raw_1, w1.rearrange("(c p) n -> p c n", p=P)).then_inc(raw_loaded[1], 16)
            sp.dma_start(raw_2, w2.rearrange("(f p) n -> p f n", p=P)).then_inc(raw_loaded[2], 16)
            for n in range(LAYERS):
                sp.dma_start(raw_l[:, n, 0], Wq[n]).then_inc(raw_loaded[3], 16)
                sp.dma_start(raw_l[:, n, 1], Wk[n]).then_inc(raw_loaded[3], 16)
                sp.dma_start(raw_l[:, n, 2:4], Wc[n].rearrange("(c p) d -> p c d", p=P)).then_inc(raw_loaded[3], 16)

            def body(i, A, H, L, T, N):
                if L:
                    wait(sp, adj_l_used, i - 2)
                    sp.dma_start(adj_l[:], adj_v[i - 2]).then_inc(adj_l_loaded, 16)
                if T:
                    wait(sp, l_out, i - 2)
                    sp.dma_start(out_v[i - 3], x3[:]).then_inc(stored, 16)
                if N:
                    wait(sp, x_used, i + 1)
                    sp.dma_start(x_in[:], x_v[i + 1]).then_inc(x_loaded, 16)
                    wait(sp, adj_a_used, i + 1)
                    sp.dma_start(adj_a[:], adj_v[i + 1]).then_inc(adj_a_loaded, 16)

            run(sp, body)
            sp.wait_ge(stored, 16 * GROUPS)

        @block.tensor
        def _(pe):
            def product(dst, lhs, rhs, terms):
                parts = [(a, b) for a, b in ((0, 0), (1, 0), (0, 1))]
                n = len(terms) * len(parts)
                k = 0
                for t in terms:
                    for a, b in parts:
                        last = nc.tensor.matmul(dst, lhs(t, a), rhs(t, b), start=(k == 0), stop=(k == n - 1))
                        k += 1
                return last

            def turn(ring, g, job, src, c):
                dst = wait_empty(pe, ring, g, job)
                for t in range(TILES):
                    last = nc.tensor.transpose(dst[:, t * P:(t + 1) * P], src[:, t, c * P:(c + 1) * P], ident[:])
                last.then_inc(is_filled(ring, job), 1)

            pe.wait_ge(consts, 2)
            pe.wait_ge(raw_loaded[0], 64)
            pe.wait_ge(params_loaded, 16 * 16)
            mm = nc.tensor.matmul
            nc.tensor.transpose(bank[7][:, 0:PARAMS], param_rows, ident[0:PARAMS, 0:PARAMS]).then_inc(prep_p, 1)
            pe.wait_ge(prep_d, 1)
            for n, w in enumerate((0, 1, 2)):
                for o in range(DC):
                    for c in range(DC):
                        last = mm(bank[0][:, 2 * n + o:2 * n + o + 1], raw_qkvo[:, w, c, o * P:(o + 1) * P],
                                  b1c[:, c:c + 1], start=(c == 0), stop=(c == DC - 1))
            pe.wait_ge(raw_loaded[1], 16)
            for f in range(FC):
                for c in range(DC):
                    last = mm(bank[0][:, 8 + f:9 + f], raw_1[:, c, f * P:(f + 1) * P], b2c[:, c:c + 1],
                              start=(c == 0), stop=(c == DC - 1))
            last.then_inc(prep_p, 1)
            pe.wait_ge(prep_d, 2)
            for c in range(DC):
                last = mm(bank[1][:, 0:D], bv_c[:, c:c + 1].to_broadcast([P, P]), raw_qkvo[:, 3, c, :],
                          start=(c == 0), stop=(c == DC - 1))
            last.then_inc(prep_p, 1)
            pe.wait_ge(raw_loaded[3], 96)
            for n in range(LAYERS):
                for w in range(2):
                    for c in range(DC):
                        last = nc.tensor.transpose(bank[2 + n][:, (w * DC + c) * P:(w * DC + c + 1) * P],
                                                   raw_l[:, n, w, c * P:(c + 1) * P], ident[:])
                for c in range(DC):
                    for e in range(DC):
                        last = nc.tensor.transpose(bank[4 + n][:, c * D + e * P:c * D + (e + 1) * P],
                                                   raw_l[:, n, 2 + e, c * P:(c + 1) * P], ident[:])
            last.then_inc(prep_p, 1)
            pe.wait_ge(prep_g, 2)
            pe.wait_ge(prep_d, 5)

            def a_turn(g):
                wait(pe, x_hat_ready, TILES * g + TILES)
                for c in range(DC):
                    turn("A", g, A_JOBS["xT"] + c, x_hat, c)

            def a_qk(g, w):
                for o in range(DC):
                    job = A_JOBS["qk"[w]] + o
                    dst = wait_sources(pe, "A", g, [A_JOBS["xT"], A_JOBS["xT"] + 1], job)
                    product(dst[:], lambda c, s: w_qkv[s][:, w, c, o * P:(o + 1) * P], lambda c, s: xT[s][:, c, :],
                            range(DC)).then_inc(is_filled("A", job), 1)

            def a_v(g):
                for k in range(2):
                    job = A_JOBS["v"] + k
                    dst = wait_empty(pe, "A", g, job)
                    for t in (2 * k, 2 * k + 1):
                        last = product(dst[:, t % 2 * D:(t % 2 + 1) * D], lambda c, s: xT[s][:, c, t * P:(t + 1) * P],
                                       lambda c, s: w_qkv[s][:, 2, c, :], range(DC))
                    last.then_inc(is_filled("A", job), 1)

            def a_scores(g, t):
                job = A_JOBS["s"] + t
                dst = wait_sources(pe, "A", g, range(A_JOBS["q"], A_JOBS["k"] + DC), job)
                for c in range(DC):
                    for b in range(2):
                        n = 2 * t + b
                        last = mm(dst[b * NODES:(b + 1) * NODES, c * 256:(c + 1) * 256],
                                  qT[:, c, n * NODES:(n + 1) * NODES],
                                  kT[:, c, n].rearrange("p j k -> p (j k)"), start=True, stop=True)
                last.then_inc(is_filled("A", job), 1)

            def a_turn_p(g, t):
                wait(pe, p_ready, TILES * g + t + 1)
                job = P_JOB[t]
                dst = wait_empty(pe, "A", g, job)
                for j in range(H0):
                    last = nc.tensor.transpose(dst[:, j * P:(j + 1) * P], sc[:, t, j * P:(j + 1) * P], ident[:])
                last.then_inc(is_filled("A", job), 1)

            H0 = 4

            def a_values(g, k):
                job = O_JOB[k]
                dst = wait_sources(pe, "A", g, [A_JOBS["v"], A_JOBS["v"] + 1, P_JOB[2 * k], P_JOB[2 * k + 1]], job)
                for t in (2 * k, 2 * k + 1):
                    for b in range(2):
                        for j in range(H0):
                            at = (t % 2) * 256 + (j // 2) * P + b * NODES
                            last = mm(dst[j % 2 * 64:j % 2 * 64 + 64, at:at + NODES],
                                      v2[:, 2 * t + b, j].rearrange("p a d -> p (a d)"),
                                      pT[:, t % 2, j * P + b * NODES:j * P + (b + 1) * NODES], start=True, stop=True)
                last.then_inc(is_filled("A", job), 1)

            def a_out(g, k):
                job = A_JOBS["w"] + k
                dst = wait_sources(pe, "A", g, [O_JOB[k]], job)
                for t in (2 * k, 2 * k + 1):
                    last = product(dst[:, t % 2 * D:(t % 2 + 1) * D], lambda c, s: oT[s][:, c, t * P:(t + 1) * P],
                                   lambda c, s: w_o[s][:, c, :], range(DC))
                last.then_inc(is_filled("A", job), 1)

            def h_turn(g):
                wait(pe, x1_hat_ready, TILES * g + TILES)
                for c in range(DC):
                    turn("M", g, M_JOBS["xT"] + c, x1_hat, c)

            def h_up(g, f):
                job = M_JOBS["h"] + f
                dst = wait_sources(pe, "M", g, [M_JOBS["xT"], M_JOBS["xT"] + 1], job)
                product(dst[:], lambda c, s: w_1[s][:, c, f * P:(f + 1) * P], lambda c, s: nT[s][:, c, :],
                        range(DC)).then_inc(is_filled("M", job), 1)

            def y_down(g, k):
                wait(pe, h_lo, FC * g + FC)
                job = M_JOBS["y"] + k
                dst = wait_empty(pe, "M", g, job)
                for t in (2 * k, 2 * k + 1):
                    last = product(dst[:, t % 2 * D:(t % 2 + 1) * D], lambda f, s: hT[s][:, f, t * P:(t + 1) * P],
                                   lambda f, s: w_2[s][:, f, :], range(FC))
                last.then_inc(is_filled("M", job), 1)

            def l_turn(g, l):
                if l == 0:
                    for k in range(2):
                        wait_drained(pe, "M", g, M_JOBS["y"] + k)
                else:
                    wait(pe, l_x, TILES * g + TILES)
                for c in range(DC):
                    turn("L", g, L_JOBS[f"xT{l}"] + c, (x2, x3)[l], c)

            def l_qk(g, l):
                for w in range(2):
                    job = L_JOBS[f"qk{l}"] + w
                    dst = wait_sources(pe, "L", g, [L_JOBS[f"xT{l}"], L_JOBS[f"xT{l}"] + 1], job)
                    product(dst[:], lambda c, s: w_l[s][:, l, w, c, :], lambda c, s: lT[s][:, c, :],
                            range(DC)).then_inc(is_filled("L", job), 1)

            def l_xw(g, l):
                for k in range(2):
                    job = L_JOBS[f"xw{l}"] + k
                    dst = wait_empty(pe, "L", g, job)
                    for t in (2 * k, 2 * k + 1):
                        last = product(dst[:, t % 2 * D:(t % 2 + 1) * D], lambda c, s: lT[s][:, c, t * P:(t + 1) * P],
                                       lambda c, s: w_c[s][:, l, c, :], range(DC))
                    last.then_inc(is_filled("L", job), 1)

            def l_scores(g, l):
                job = L_JOBS[f"s{l}"]
                dst = wait_sources(pe, "L", g, [L_JOBS[f"qk{l}"], L_JOBS[f"qk{l}"] + 1], job)
                for t in range(TILES):
                    at = slice(t * P, (t + 1) * P)
                    last = mm(dst[:, at], lqk[:, 0, at], lqk[:, 1, at], start=True, stop=True)
                last.then_inc(is_filled("L", job), 1)

            def l_turn_p(g, l):
                job = L_JOBS[f"p{l}"]
                dst = wait_empty(pe, "L", g, job)
                for t in range(TILES):
                    wait(pe, l_exp, 2 * TILES * g + TILES * l + t + 1)
                    last = nc.tensor.transpose(dst[:, t * P:(t + 1) * P], ls[:, t], ident[:])
                last.then_inc(is_filled("L", job), 1)

            def l_mix(g, l):
                for k in range(2):
                    job = L_JOBS[f"o{l}"] + k
                    sources = [L_JOBS[f"p{l}"], L_JOBS[f"xw{l}"], L_JOBS[f"xw{l}"] + 1]
                    dst = wait_sources(pe, "L", g, sources, job)
                    for t in (2 * k, 2 * k + 1):
                        last = mm(dst[:, t % 2 * D:(t % 2 + 1) * D], lpT[:, t], lxw[:, t], start=True, stop=True)
                    last.then_inc(is_filled("L", job), 1)

            def body(i, A, H, L, T, N):
                if A:
                    a_turn(i)
                if L:
                    y_down(i - 2, 0)
                if T:
                    l_turn_p(i - 3, 1)
                if A:
                    a_qk(i, 0)
                if T:
                    l_mix(i - 3, 1)
                if A:
                    a_qk(i, 1)
                if L:
                    y_down(i - 2, 1)
                if A:
                    a_v(i)
                    a_scores(i, 0)
                    a_scores(i, 1)
                if L:
                    l_turn(i - 2, 0)
                if A:
                    a_scores(i, 2)
                    a_scores(i, 3)
                if H:
                    h_turn(i - 1)
                    h_up(i - 1, 0)
                    h_up(i - 1, 1)
                if L:
                    l_qk(i - 2, 0)
                    l_xw(i - 2, 0)
                if A:
                    a_turn_p(i, 0)
                    a_turn_p(i, 1)
                if H:
                    h_up(i - 1, 2)
                if A:
                    a_values(i, 0)
                if L:
                    l_scores(i - 2, 0)
                if H:
                    h_up(i - 1, 3)
                if A:
                    a_turn_p(i, 2)
                    a_turn_p(i, 3)
                if H:
                    h_up(i - 1, 4)
                if A:
                    a_values(i, 1)
                if L:
                    l_turn_p(i - 2, 0)
                if A:
                    a_out(i, 0)
                if L:
                    l_mix(i - 2, 0)
                if H:
                    h_up(i - 1, 5)
                if A:
                    a_out(i, 1)
                if H:
                    h_up(i - 1, 6)
                if L:
                    l_turn(i - 2, 1)
                if H:
                    h_up(i - 1, 7)
                if L:
                    l_qk(i - 2, 1)
                    l_xw(i - 2, 1)
                    l_scores(i - 2, 1)

            run(pe, body)

        @block.scalar
        def _(act):
            act.wait_ge(prep_d, 5)
            act.wait_ge(prep_p, 4)
            act.wait_ge(prep_g, 2)

            def a_hi(g):
                for c in range(DC):
                    src = wait_filled(act, "A", g, A_JOBS["xT"] + c)
                    nc.scalar.activation(xT[0][:, c], src[:], ACT.Identity).then_inc(hi_a, 1)

            def a_qk(g):
                for c in range(DC):
                    job = A_JOBS["q"] + c
                    src = wait_filled(act, "A", g, job)
                    nc.scalar.activation(qT[:, c], src[:], ACT.Identity, bias=bq_c[:, c:c + 1],
                                         scale=SCALE0).then_inc(is_drained("A", job), 1)
                for c in range(DC):
                    job = A_JOBS["k"] + c
                    src = wait_filled(act, "A", g, job)
                    for j in range(QUADS):
                        at = slice(j * HD, (j + 1) * HD)
                        last = nc.scalar.activation(kT[at, c, :, j, :], src[at, :].rearrange("p (g k) -> p g k", k=NODES),
                                                    ACT.Identity, bias=bk_c[at, c:c + 1])
                    last.then_inc(is_drained("A", job), 1)

            def a_v(g):
                for k in range(2):
                    job = A_JOBS["v"] + k
                    src = wait_filled(act, "A", g, job)[:].rearrange("p (t j a d) -> p t j a d", t=2, a=2, d=HD)
                    for b in range(2):
                        for a in range(2):
                            dst = v2[a * 64:(a + 1) * 64].rearrange("p (t b) j a d -> p t b j a d", b=2)
                            last = nc.scalar.activation(dst[:, 2 * k:2 * k + 2, b, :, a, :],
                                                        src[b * 64:(b + 1) * 64, :, :, a, :], ACT.Identity)
                    last.then_inc(is_drained("A", job), 1)

            def a_exp(g, t):
                wait(act, shifted, TILES * g + t + 1)
                nc.scalar.activation(sc[:, t], sc[:, t], ACT.Exp).then_inc(exp_done, 1)

            def a_copy_p(g, t):
                src = wait_filled(act, "A", g, P_JOB[t])
                nc.scalar.activation(pT[:, t % 2], src[:], ACT.Identity).then_inc(is_drained("A", P_JOB[t]), 1)

            def a_hi_o(g, k):
                src = wait_filled(act, "A", g, O_JOB[k])[:].rearrange("p (t c r) -> p t c r", t=2, c=DC)
                dst = oT[0][:].rearrange("p c (t r) -> p t c r", r=P)[:, 2 * k:2 * k + 2]
                nc.scalar.activation(dst, src, ACT.Identity).then_inc(hi_a, 1)

            def h_hi_x(g):
                for c in range(DC):
                    src = wait_filled(act, "M", g, M_JOBS["xT"] + c)
                    nc.scalar.activation(nT[0][:, c], src[:], ACT.Identity).then_inc(hi_m, 1)

            def h_gelu(g, f):
                wait(act, h_lo, FC * g + max(f - HB + 1, 0))
                job = M_JOBS["h"] + f
                src = wait_filled(act, "M", g, job)
                nc.scalar.activation(hf[:, f % HB], src[:], ACT.Gelu, bias=bh_c[:, f:f + 1])
                nc.scalar.activation(hT[0][:, f], src[:], ACT.Gelu, bias=bh_c[:, f:f + 1])\
                    .then_inc(is_drained("M", job), 1)

            def l_hi(g, l):
                for c in range(DC):
                    src = wait_filled(act, "L", g, L_JOBS[f"xT{l}"] + c)
                    nc.scalar.activation(lT[0][:, c], src[:], ACT.Identity).then_inc(hi_l, 1)

            def l_copies(g, l):
                for w in range(2):
                    job = L_JOBS[f"qk{l}"] + w
                    src = wait_filled(act, "L", g, job)
                    nc.scalar.activation(lqk[:, w], src[:], ACT.Identity, bias=(lq_c, lk_c)[w][:, l:l + 1],
                                         scale=(SCALE1, 1.0)[w]).then_inc(is_drained("L", job), 1)
                for k in range(2):
                    job = L_JOBS[f"xw{l}"] + k
                    src = wait_filled(act, "L", g, job)
                    nc.scalar.activation(lxw[:, 2 * k:2 * k + 2].rearrange("p t d -> p (t d)"), src[:], ACT.Identity)\
                        .then_inc(is_drained("L", job), 1)

            def l_exps(g, l):
                wait(act, l_top, 2 * g + l + 1)
                for t in range(TILES):
                    nc.scalar.activation(ls[:, t], ls[:, t], ACT.Exp, bias=ltop[:, t:t + 1],
                                         accum_out=lsum[:, t:t + 1]).then_inc(l_exp, 1)

            def l_copy_p(g, l):
                job = L_JOBS[f"p{l}"]
                src = wait_filled(act, "L", g, job)
                nc.scalar.activation(lqk[:, 0, :], src[:], ACT.Identity)\
                    .then_inc(is_drained("L", job), 1)

            def body(i, A, H, L, T, N):
                if A:
                    a_hi(i)
                if T:
                    l_copy_p(i - 3, 1)
                if A:
                    a_qk(i)
                    a_v(i)
                    a_exp(i, 0)
                if L:
                    l_hi(i - 2, 0)
                if A:
                    a_exp(i, 1)
                if H:
                    h_hi_x(i - 1)
                    h_gelu(i - 1, 0)
                    h_gelu(i - 1, 1)
                if A:
                    a_exp(i, 2)
                if L:
                    l_copies(i - 2, 0)
                if A:
                    a_copy_p(i, 0)
                    a_copy_p(i, 1)
                    a_exp(i, 3)
                if H:
                    h_gelu(i - 1, 2)
                if A:
                    a_hi_o(i, 0)
                if H:
                    h_gelu(i - 1, 3)
                if L:
                    l_exps(i - 2, 0)
                if A:
                    a_copy_p(i, 2)
                    a_copy_p(i, 3)
                if H:
                    h_gelu(i - 1, 4)
                if A:
                    a_hi_o(i, 1)
                if L:
                    l_copy_p(i - 2, 0)
                if H:
                    h_gelu(i - 1, 5)
                    h_gelu(i - 1, 6)
                if L:
                    l_hi(i - 2, 1)
                if H:
                    h_gelu(i - 1, 7)
                if L:
                    l_copies(i - 2, 1)
                    l_exps(i - 2, 1)

            run(act, body)

        @block.gpsimd
        def _(pool):
            nc.gpsimd.memset(ident[:], 0.0).then_inc(consts, 1)
            pool.wait_ge(consts, 1)
            nc.gpsimd.affine_select(out=ident[:], in_=ident[:], compare_op=ALU.not_equal, fill=1.0, base=0,
                                    pattern=[[-1, P]], channel_multiplier=1).then_inc(consts, 1)
            nc.gpsimd.memset(minus_half, -0.5)
            nc.gpsimd.memset(pen1[:], MASKED)
            pool.wait_ge(prep_d, 5)
            pool.wait_ge(prep_p, 4)
            nc.gpsimd.memset(kT[:], 0.0).then_inc(prep_g, 1)
            nc.gpsimd.memset(v2[:], 0.0).then_inc(prep_g, 1)
            pool.wait_ge(prep_g, 2)

            def normalise(g, s, src, dst, chain, ready):
                _, _, nm, ve, rs = stats[s]
                wait(pool, {"A": stats_a, "H": stats_h}[s], 2 * g + 2)
                nc.gpsimd.tensor_tensor(rs[:], ve[:], minus_half, ALU.pow).then_inc(chain, 1)
                wait(pool, chain, g + 1)
                nc.gpsimd.tensor_tensor(spare_p, minus_half[:, 0:1], minus_half[:, 0:1], ALU.add)
                for t in range(TILES):
                    nc.gpsimd.tensor_scalar(dst[:, t], src[:, t], nm[:, t:t + 1], rs[:, t:t + 1], ALU.add,
                                            ALU.mult).then_inc(ready, 1)

            def a_normalise(g):
                normalise(g, "A", x_in, x_hat, pool_a, x_hat_ready)

            def a_add_bo(g):
                wait(pool, x1_b2_ready, g)
                wait(pool, x1_hat_ready, TILES * g)
                nc.gpsimd.tensor_tensor(x1[:], x_in[:], bo_row[:].rearrange("p (t d) -> p t d", t=1)
                                        .to_broadcast([P, TILES, D]), ALU.add).then_inc(x1_begun, 1)
                wait(pool, x1_begun, g + 1)
                pool.sem_inc(x_used, 1)

            def h_normalise(g):
                normalise(g, "H", x1, x1_hat, pool_h, x1_hat_ready)

            def h_add_b2(g):
                for k in range(2):
                    wait_all_drained_before(pool, "M", g, M_JOBS["y"] + k)
                nc.gpsimd.tensor_tensor(x1_b2[:], x1[:], b2_row[:].rearrange("p (t d) -> p t d", t=1)
                                        .to_broadcast([P, TILES, D]), ALU.add).then_inc(x1_b2_ready, 1)

            def l_rstd(g, l):
                _, _, nm, ve, rs = stats["L"]
                wait(pool, stats_l, 2 * (2 * g + l + 1))
                nc.gpsimd.tensor_tensor(rs[:], ve[:], minus_half, ALU.pow).then_inc(rstd_l, 1)

            def body(i, A, H, L, T, N):
                if H:
                    if A:
                        for c in range(DC):
                            wait_filled(pool, "A", i, A_JOBS["xT"] + c)
                    h_normalise(i - 1)
                if T:
                    l_rstd(i - 3, 1)
                if H:
                    h_add_b2(i - 1)
                if A:
                    a_add_bo(i)
                if N:
                    a_normalise(i + 1)
                if L:
                    l_rstd(i - 2, 0)

            a_normalise(0)
            run(pool, body)

        @block.vector
        def _(dve):
            tt = nc.vector.tensor_tensor
            ts = nc.vector.tensor_scalar
            stt = nc.vector.scalar_tensor_tensor
            dve.wait_ge(params_loaded, 16 * 16)
            dve.wait_ge(prep_p, 1)
            nc.vector.tensor_copy(cols[:, 0:PARAMS], bank[7][:, 0:PARAMS]).then_inc(prep_d, 1)
            dve.wait_ge(prep_d, 1)
            dve.wait_ge(prep_p, 2)
            tt(cols[:, 8:14], cols[:, 8:14], bank[0][:, 0:6], ALU.add)
            tt(bh_c, bh_c, bank[0][:, 8:16], ALU.add).then_inc(prep_d, 1)
            dve.wait_ge(prep_d, 2)
            ts(bq_c, bq_c, SCALE0, None, ALU.mult)
            ts(lq_c, lq_c, SCALE1, None, ALU.mult)
            dve.wait_ge(prep_p, 3)
            tt(bo_row[:], bo_row[:], bank[1][:, 0:D], ALU.add).then_inc(prep_d, 1)
            dve.wait_ge(raw_loaded[1], 16)
            dve.wait_ge(raw_loaded[2], 16)
            for c in range(DC):
                ts(raw_qkvo[:, 0:3, c], raw_qkvo[:, 0:3, c], g1c[:, c:c + 1], None, ALU.mult)
                ts(raw_1[:, c], raw_1[:, c], g2c[:, c:c + 1], None, ALU.mult).then_inc(prep_a, 1)
            dve.wait_ge(prep_a, 2)
            dve.wait_ge(prep_p, 4)
            pairs = [(raw_qkvo[:, 0:3], w_qkv, slice(None)), (raw_qkvo[:, 3], w_o, slice(None)),
                     (raw_1, w_1, slice(None)), (raw_2, w_2, slice(None))]
            for n in range(LAYERS):
                pairs.append((bank[2 + n][:].rearrange("p (w c f) -> p w c f", w=2, c=DC),
                              (w_l[0][:, n], w_l[1][:, n]), None))
                pairs.append((bank[4 + n][:].rearrange("p (c d) -> p c d", c=DC), (w_c[0][:, n], w_c[1][:, n]), None))
            views = [(src, parts[0] if at is None else parts[0][:], parts[1] if at is None else parts[1][:])
                     for src, parts, at in pairs]
            for src, hi, lo in views:
                last = nc.vector.tensor_copy(hi, src)
            last.then_inc(prep_d, 1)
            dve.wait_ge(prep_d, 4)
            for src, hi, lo in views:
                last = tt(lo, src, hi.bitcast(F32), ALU.subtract)
            last.then_inc(prep_d, 1)

            class Chain:

                def __init__(self, s, per_group, g, n=0):
                    self.s, self.base, self.n = s, g * per_group, n

                def step(self, ins):
                    self.n += 1
                    ins.then_inc(self.s, 1)

                def wait(self):
                    wait(dve, self.s, self.base + self.n)

            def norm_stats(s, src, chain, ready):
                st, mv, nm, ve, rs = stats[s]
                for t in range(TILES):
                    ins = nc.vector.bn_stats(st[:, t], src[:, t])
                chain.step(ins)
                chain.wait()
                nc.vector.memset(spare_d, 0.0)
                for t in range(TILES):
                    ins = nc.vector.bn_aggr(mv[:, t], st[:, t])
                chain.step(ins)
                chain.wait()
                ts(nm[:], mv[:, :, 0], -1.0, None, ALU.mult).then_inc(ready, 1)
                ts(ve[:], mv[:, :, 1], EPS, None, ALU.add).then_inc(ready, 1)

            N_STEPS = 2
            A_STEPS = 1 + 3 * TILES
            H_STEPS = 2
            L_STEPS = LAYERS * 4

            def a_norm(g, ch):
                wait(dve, x_loaded, 16 * g + 16)
                norm_stats("A", x_in, ch, stats_a)

            def a_edges(g, ch):
                wait(dve, adj_a_loaded, 16 * g + 16)
                stt(bias0[:], adj_a[:], 0.1, adj_a[:], ALU.mult, ALU.mult)
                ts(pen[:], adj_a[:], 0, MASKED, ALU.is_le, ALU.mult).then_inc(adj_a_used, 1)
                wait(dve, adj_a_used, g + 1)
                ch.step(tt(bias0[:], bias0[:], pen[:], ALU.add))

            def lo_of(ring, g, job, hi_sem, count, hi, lo, view=None):
                src = wait_filled(dve, ring, g, job)[:]
                if view:
                    src = view(src)
                wait(dve, hi_sem, count)
                tt(lo, src, hi.bitcast(F32), ALU.subtract).then_inc(is_drained(ring, job), 1)

            def a_lo(g):
                for c in range(DC):
                    lo_of("A", g, A_JOBS["xT"] + c, hi_a, 4 * g + c + 1, xT[0][:, c], xT[1][:, c])

            heads = lambda a: a.rearrange("p (h k) -> p h k", h=H)
            spread = lambda a: a.rearrange("p (h k) -> p h k", k=1).to_broadcast([P, H, NODES])

            def a_front(g, t, ch):
                job = A_JOBS["s"] + t
                src = wait_filled(dve, "A", g, job)
                s = heads(sc[:, t])
                if t == 0:
                    ch.wait()
                tt(s, heads(src[:]), bias0[:, t].rearrange("p (h k) -> p h k", h=1).to_broadcast([P, H, NODES]),
                   ALU.add).then_inc(is_drained("A", job), 1)
                wait_drained(dve, "A", g, job)
                ch.step(nc.vector.reduce_max(top[:, t], s, AX_X))
                ch.wait()
                tt(s, s, spread(top[:, t]), ALU.subtract).then_inc(shifted, 1)

            def a_back(g, t, ch):
                wait(dve, exp_done, TILES * g + t + 1)
                e = heads(sc[:, t])
                ch.step(nc.vector.reduce_sum(total[:, t], e, AX_X))
                ch.wait()
                ch.step(nc.vector.reciprocal(share[:, t], total[:, t]))
                ch.wait()
                tt(heads(sc[:, t]), e, spread(share[:, t]), ALU.mult).then_inc(p_ready, 1)

            def a_lo_o(g, k):
                dst = [oT[s][:].rearrange("p c (t r) -> p t c r", r=P)[:, 2 * k:2 * k + 2] for s in range(2)]
                lo_of("A", g, O_JOB[k], hi_a, 4 * g + 3 + k, dst[0], dst[1],
                      lambda b: b.rearrange("p (t c r) -> p t c r", t=2, c=DC))

            def a_residual(g, k):
                if k == 0:
                    wait(dve, x1_begun, g + 1)
                job = A_JOBS["w"] + k
                src = wait_filled(dve, "A", g, job)
                tt(x1[:, 2 * k:2 * k + 2], src[:].rearrange("p (t d) -> p t d", t=2), x1[:, 2 * k:2 * k + 2],
                   ALU.add).then_inc(is_drained("A", job), 1)

            def h_norm(g, ch):
                for k in range(2):
                    wait_drained(dve, "A", g, A_JOBS["w"] + k)
                norm_stats("H", x1, ch, stats_h)

            def h_lo_x(g):
                for c in range(DC):
                    lo_of("M", g, M_JOBS["xT"] + c, hi_m, DC * g + c + 1, nT[0][:, c], nT[1][:, c])

            def h_rest(g, f):
                wait_drained(dve, "M", g, M_JOBS["h"] + f)
                tt(hT[1][:, f], hf[:, f % HB], hT[0][:, f].bitcast(F32), ALU.subtract).then_inc(h_lo, 1)

            def y_residual(g, k):
                if k == 0:
                    wait(dve, x1_b2_ready, g + 1)
                job = M_JOBS["y"] + k
                src = wait_filled(dve, "M", g, job)
                tt(x2[:, 2 * k:2 * k + 2], src[:].rearrange("p (t d) -> p t d", t=2), x1_b2[:, 2 * k:2 * k + 2],
                   ALU.add).then_inc(is_drained("M", job), 1)

            def l_mask(g):
                wait(dve, adj_l_loaded, 16 * g + 16)
                for b in range(2):
                    at = slice(b * NODES, (b + 1) * NODES)
                    ins = ts(pen1[at, :, b, :], adj_l[at], 0, MASKED, ALU.is_equal, ALU.mult)
                ins.then_inc(adj_l_used, 1)
                wait(dve, adj_l_used, g + 1)

            def l_lo(g, l):
                for c in range(DC):
                    lo_of("L", g, L_JOBS[f"xT{l}"] + c, hi_l, 2 * DC * g + DC * l + c + 1, lT[0][:, c], lT[1][:, c])

            def l_front(g, l, ch):
                job = L_JOBS[f"s{l}"]
                src = wait_filled(dve, "L", g, job)
                tt(ls[:].rearrange("p t n -> p (t n)"), src[:], pen1[:].rearrange("p t b k -> p (t b k)"),
                   ALU.add).then_inc(is_drained("L", job), 1)
                wait_drained(dve, "L", g, job)
                nc.vector.tensor_reduce(ltop[:], ls[:], AX_X, ALU.max, negate=True).then_inc(l_top, 1)

            def l_mix(g, l, ch):
                wait(dve, l_exp, 2 * TILES * g + TILES * (l + 1))
                ch.step(nc.vector.reciprocal(lshare[:], lsum[:]))
                ch.wait()
                prev = (x2, x3)[l]
                if l == 0:
                    for k in range(2):
                        wait_drained(dve, "M", g, M_JOBS["y"] + k)
                for t in range(TILES):
                    job = L_JOBS[f"o{l}"] + t // 2
                    src = wait_filled(dve, "L", g, job) if t % 2 == 0 else src
                    ins = stt(prev[:, t], src[:, t % 2 * D:(t % 2 + 1) * D], lshare[:, t:t + 1], prev[:, t], ALU.mult,
                              ALU.add)
                    if t % 2:
                        ins.then_inc(is_drained("L", job), 1)
                for k in range(2):
                    wait_drained(dve, "L", g, L_JOBS[f"o{l}"] + k)
                norm_stats("L", prev, ch, stats_l)

            def l_norm(g, l, ch):
                prev = (x2, x3)[l]
                _, _, nm, ve, rs = stats["L"]
                wait(dve, stats_l, 2 * (2 * g + l + 1))
                for t in range(TILES):
                    ins = stt(prev[:, t], prev[:, t], nm[:, t:t + 1], lg_row[:, l], ALU.add, ALU.mult)
                ch.step(ins)
                wait(dve, rstd_l, 2 * g + l + 1)
                ch.wait()
                if l == 0:
                    wait(dve, stored, 16 * g)
                for t in range(TILES):
                    ins = stt(x3[:, t], prev[:, t], rs[:, t:t + 1], lb_row[:, l], ALU.mult, ALU.add)
                    if l == 0:
                        ins.then_inc(l_x, 1)
                if l == 1:
                    ins.then_inc(l_out, 1)
                else:
                    wait(dve, l_x, TILES * g + TILES)

            def body(i, A, H, L, T, N):
                ca = Chain(dve_a, A_STEPS, i)
                cn = Chain(dve_n, N_STEPS, i + 1)
                chh = Chain(dve_h, H_STEPS, i - 1)
                cl = Chain(dve_l, L_STEPS, i - 2)
                ct = Chain(dve_l, L_STEPS, i - 3, L_STEPS // 2)
                if A:
                    a_lo(i)
                if H:
                    h_norm(i - 1, chh)
                if L:
                    y_residual(i - 2, 0)
                if A:
                    a_edges(i, ca)
                if L:
                    l_mask(i - 2)
                if T:
                    l_mix(i - 3, 1, ct)
                if L:
                    y_residual(i - 2, 1)
                if T:
                    l_norm(i - 3, 1, ct)
                if A:
                    a_front(i, 0, ca)
                    a_front(i, 1, ca)
                if L:
                    l_lo(i - 2, 0)
                if A:
                    a_back(i, 0, ca)
                if H:
                    h_lo_x(i - 1)
                if A:
                    a_front(i, 2, ca)
                if H:
                    h_rest(i - 1, 0)
                if A:
                    a_back(i, 1, ca)
                if H:
                    h_rest(i - 1, 1)
                if A:
                    a_front(i, 3, ca)
                    a_back(i, 2, ca)
                if H:
                    h_rest(i - 1, 2)
                if A:
                    a_back(i, 3, ca)
                if L:
                    l_front(i - 2, 0, cl)
                if H:
                    h_rest(i - 1, 3)
                if N:
                    a_norm(i + 1, cn)
                if A:
                    a_lo_o(i, 0)
                if L:
                    l_mix(i - 2, 0, cl)
                if H:
                    h_rest(i - 1, 4)
                if A:
                    a_lo_o(i, 1)
                if L:
                    l_norm(i - 2, 0, cl)
                if A:
                    a_residual(i, 0)
                if H:
                    h_rest(i - 1, 5)
                if A:
                    a_residual(i, 1)
                if H:
                    h_rest(i - 1, 6)
                if L:
                    l_lo(i - 2, 1)
                if H:
                    h_rest(i - 1, 7)
                if L:
                    l_front(i - 2, 1, cl)
                assert not A or ca.n == A_STEPS
                assert not N or cn.n == N_STEPS
                assert not H or chh.n == H_STEPS
                assert not L or cl.n == L_STEPS // 2
                assert not T or ct.n == L_STEPS

            a_norm(0, Chain(dve_n, N_STEPS, 0))
            run(dve, body)


_INS = ['x', 'adj', 'L0_gnn_ln1_g', 'L0_gnn_ln1_b', 'L0_gnn_ln2_g', 'L0_gnn_ln2_b', 'L0_gnn_wq', 'L0_gnn_bq',
        'L0_gnn_wk', 'L0_gnn_bk', 'L0_gnn_wv', 'L0_gnn_bv', 'L0_gnn_wo', 'L0_gnn_bo', 'L0_gnn_w1', 'L0_gnn_b1',
        'L0_gnn_w2', 'L0_gnn_b2', 'L1_gnn_Wq', 'L1_gnn_bq', 'L1_gnn_Wk', 'L1_gnn_bk', 'L1_gnn_Wc', 'L1_gnn_ln_g',
        'L1_gnn_ln_b']


def kernel(**inputs):
    import numpy as _np
    import concourse.bacc as _bacc
    from concourse import mybir as _mybir
    from concourse.bass_utils import run_bass_kernel_spmd as _run

    nc = _bacc.Bacc("TRN2", target_bir_lowering=False, num_devices=1)
    arrays, args = {}, []
    for name in _INS:
        a = _np.ascontiguousarray(inputs[name])
        arrays[f"in_{name}_dram"] = a
        args.append(nc.dram_tensor(f"in_{name}_dram", a.shape, _mybir.dt.from_np(a.dtype), kind="ExternalInput").ap())
    shape = arrays["in_x_dram"].shape
    args.append(nc.dram_tensor("out_0_dram", shape, _mybir.dt.float32, kind="ExternalOutput").ap())
    gnn_kernel(nc, *args)
    r = _run(nc, [arrays], core_ids=[0])
    return r.results[0]["out_0_dram"]
```

```python
from contextlib import ExitStack

import concourse.bass as bass
from concourse import mybir

P = 128
TILES = 4
ROWS = TILES * P
NODES = 64
GRAPHS = ROWS // NODES
EPS = 1e-5
MASKED = -1e30

ALU = mybir.AluOpType
ACT = mybir.ActivationFunctionType
F32 = mybir.dt.float32
F32R = mybir.dt.float32r
I32 = mybir.dt.int32
AX_X = mybir.AxisListType.X


def number(jobs):
    first, n = {}, 0
    for name, count in jobs:
        first[name] = n
        n += count
    return first, n


A_JOBS, A_COUNT = number([("xT", 2), ("q", 2), ("k", 2), ("v", 2), ("s", 4), ("p01", 2), ("o01", 1),
                          ("p23", 2), ("o23", 1), ("w", 2)])
M_JOBS, M_COUNT = number([("xT", 2), ("h", 8), ("y", 2)])
L_JOBS, L_COUNT = number([(f"{name}{layer}", count) for layer in range(2)
                          for name, count in (("xT", 2), ("qk", 2), ("xw", 2), ("s", 1), ("p", 1), ("o", 2))])
RING = {"A": 4, "M": 2, "L": 2}
COUNT = {"A": A_COUNT, "M": M_COUNT, "L": L_COUNT}
BASE = {"A": 0, "M": 4, "L": 6}
assert all(COUNT[s] % RING[s] == 0 for s in RING)
P_JOB = [A_JOBS["p01"], A_JOBS["p01"] + 1, A_JOBS["p23"], A_JOBS["p23"] + 1]
O_JOB = [A_JOBS["o01"], A_JOBS["o23"]]


def gnn_kernel(nc, x, adj, ln1_g, ln1_b, ln2_g, ln2_b, wq, bq, wk, bk, wv, bv, wo, bo, w1, b1, w2, b2,
               Wq, bq1, Wk, bk1, Wc, ln_g, ln_b, out):
    B, S, D = x.shape
    F = w1.shape[1]
    FF = Wq.shape[1]
    DC = D // P
    FC = F // P
    H = 8
    HD = D // H
    QUADS = P // HD
    GROUPS = B * S // ROWS
    LAYERS = Wq.shape[0]
    assert S == NODES and D == 256 and HD == 32 and FF == P and LAYERS == 2 and H * NODES == 512
    SCALE0 = float(HD) ** -0.5
    SCALE1 = float(FF) ** -0.5

    x_v = x.rearrange("(G t b) s d -> G (b s) t d", t=TILES, b=2)
    adj_v = adj.rearrange("(G t b) s k -> G (b s) t k", t=TILES, b=2)
    out_v = out.rearrange("(G t b) s d -> G (b s) t d", t=TILES, b=2)

    with ExitStack() as ctx:
        def sb(name, shape, dt=F32):
            return ctx.enter_context(nc.sbuf_tensor(name, shape, dt))

        def sem(name):
            return ctx.enter_context(nc.semaphore(name))

        def split(name, shape):
            return sb(name + "_hi", shape, F32R), sb(name + "_lo", shape, F32R)

        bank = [ctx.enter_context(nc.psum_tensor(f"bank{n}", [P, 512], F32)) for n in range(8)]
        filled = [sem(f"filled{n}") for n in range(8)]
        drained = [sem(f"drained{n}") for n in range(8)]

        w_qkv = split("w_qkv", [P, 3, DC, D])
        w_o = split("w_o", [P, DC, D])
        w_1 = split("w_1", [P, DC, F])
        w_2 = split("w_2", [P, FC, D])
        w_l = split("w_l", [P, LAYERS, 2, DC, FF])
        w_c = split("w_c", [P, LAYERS, DC, D])
        ident = sb("ident", [P, P])
        cols = sb("cols", [P, 40])
        g1c, b1c, g2c, b2c = (cols[:, 2 * n:2 * n + 2] for n in range(4))
        bq_c, bk_c, bv_c = (cols[:, 8 + 2 * n:10 + 2 * n] for n in range(3))
        bh_c = cols[:, 14:22]
        lq_c, lk_c = cols[:, 22:24], cols[:, 24:26]
        bo_row = sb("bo_row", [P, D])
        b2_row = sb("b2_row", [P, D])
        lg_row = sb("lg_row", [P, LAYERS, D])
        lb_row = sb("lb_row", [P, LAYERS, D])
        spare_d, spare_p = cols[:, 26:27], cols[:, 27:28]
        minus_half = cols[:, 28:32]

        x_in = sb("x_in", [P, TILES, D])
        adj_a = sb("adj_a", [P, TILES, NODES], I32)
        pen = sb("pen", [P, TILES, NODES])
        bias0 = sb("bias0", [P, TILES, NODES])
        x_hat = sb("x_hat", [P, TILES, D])
        xT = split("xT", [P, DC, ROWS])
        qT = sb("qT", [P, DC, ROWS])
        kT = sb("kT", [P, DC, GRAPHS, QUADS, NODES])
        v2 = sb("v2", [P, GRAPHS, H // 2, 2, HD])
        top = sb("top", [P, TILES, H])
        total = sb("total", [P, TILES, H])
        share = sb("share", [P, TILES, H])
        sc = sb("sc", [P, TILES, 512])
        pT = qT
        oT = xT
        x1 = sb("x1", [P, TILES, D])
        x1_hat = x_hat
        x1_b2 = sb("x1_b2", [P, TILES, D])
        nT = split("nT", [P, DC, ROWS])
        HB = 2
        hf = sb("hf", [P, HB, ROWS])
        hT = split("hT", [P, FC, ROWS])
        x2 = sb("x2", [P, TILES, D])
        adj_l = sb("adj_l", [P, TILES, NODES], I32)
        pen1 = sb("pen1", [P, TILES, 2, NODES])
        lT = split("lT", [P, DC, ROWS])
        lqk = sb("lqk", [P, 2, ROWS])
        lxw = sb("lxw", [P, TILES, D])
        ls = sb("ls", [P, TILES, P])
        lpT = lqk[:, 0, :].rearrange("p (t n) -> p t n", t=TILES)
        ltop = sb("ltop", [P, TILES])
        lsum = sb("lsum", [P, TILES])
        lshare = sb("lshare", [P, TILES])
        x3 = sb("x3", [P, TILES, D])
        stats = {s: (sb(f"st_{s}", [P, TILES, 6]), sb(f"mv_{s}", [P, TILES, 2]), sb(f"nm_{s}", [P, TILES]),
                     sb(f"ve_{s}", [P, TILES]), sb(f"rs_{s}", [P, TILES])) for s in "AHL"}

        params_loaded = sem("params_loaded")
        raw_loaded = [sem(f"raw_loaded{n}") for n in range(5)]
        consts = sem("consts")
        prep_d = sem("prep_d")
        prep_p = sem("prep_p")
        prep_a = sem("prep_a")
        prep_g = sem("prep_g")
        x_loaded = sem("x_loaded")
        x_used = sem("x_used")
        adj_a_loaded = sem("adj_a_loaded")
        adj_a_used = sem("adj_a_used")
        adj_l_loaded = sem("adj_l_loaded")
        adj_l_used = sem("adj_l_used")
        stored = sem("stored")
        dve_n, dve_a, dve_h, dve_l = sem("dve_n"), sem("dve_a"), sem("dve_h"), sem("dve_l")
        pool_a, pool_h = sem("pool_a"), sem("pool_h")
        stats_a, stats_h, stats_l = sem("stats_a"), sem("stats_h"), sem("stats_l")
        rstd_l = sem("rstd_l")
        x_hat_ready, x1_hat_ready = sem("x_hat_ready"), sem("x1_hat_ready")
        x1_begun, x1_b2_ready = sem("x1_begun"), sem("x1_b2_ready")
        hi_a, hi_m, hi_l = sem("hi_a"), sem("hi_m"), sem("hi_l")
        shifted, exp_done, p_ready = sem("shifted"), sem("exp_done"), sem("p_ready")
        h_lo = sem("h_lo")
        l_top, l_exp, l_x, l_out = sem("l_top"), sem("l_exp"), sem("l_x"), sem("l_out")

        def wait(eng, s, value):
            if not isinstance(value, int) or value > 0:
                eng.wait_ge(s, value)

        def wait_filled(eng, ring, g, job):
            n = BASE[ring] + job % RING[ring]
            wait(eng, filled[n], g * (COUNT[ring] // RING[ring]) + job // RING[ring] + 1)
            return bank[n]

        def wait_drained(eng, ring, g, job):
            wait(eng, drained[BASE[ring] + job % RING[ring]], g * (COUNT[ring] // RING[ring]) + job // RING[ring] + 1)

        def wait_sources(eng, ring, g, sources, job):
            uses = {job % RING[ring]: job // RING[ring]}
            for n in sources:
                uses[n % RING[ring]] = max(uses.get(n % RING[ring], 0), n // RING[ring] + 1)
            for n, count in uses.items():
                wait(eng, drained[BASE[ring] + n], g * (COUNT[ring] // RING[ring]) + count)
            return bank[BASE[ring] + job % RING[ring]]

        def wait_all_drained_before(eng, ring, g, job):
            wait(eng, drained[BASE[ring] + job % RING[ring]], g * (COUNT[ring] // RING[ring])
                 - (COUNT[ring] - 1 - job) // RING[ring])

        def wait_empty(eng, ring, g, job):
            n = BASE[ring] + job % RING[ring]
            wait(eng, drained[n], g * (COUNT[ring] // RING[ring]) + job // RING[ring])
            return bank[n]

        def is_filled(ring, job):
            return filled[BASE[ring] + job % RING[ring]]

        def is_drained(ring, job):
            return drained[BASE[ring] + job % RING[ring]]

        def on(g):
            return not isinstance(g, int) or 0 <= g < GROUPS

        def run(eng, body):
            for i in range(-1, 3):
                body(i)
            with eng.Fori(3, GROUPS - 1) as i:
                body(i)
            for i in range(GROUPS - 1, GROUPS + 3):
                body(i)

        raw_qkvo = sc[:, :, :].rearrange("p t n -> p (t n)").rearrange("p (w c n) -> p w c n", w=4, c=DC)
        raw_1 = kT[:, 0].rearrange("p g j k -> p (g j k)").rearrange("p (c n) -> p c n", c=DC)
        raw_2 = kT[:, 1].rearrange("p g j k -> p (g j k)").rearrange("p (f n) -> p f n", f=FC)
        raw_l = v2[:, :, :, :, :].rearrange("p g j a d -> p (g j a d)").rearrange("p (l w e) -> p l w e", l=LAYERS, w=4)

        PARAMS = 26
        param_rows = ls[0:PARAMS, 0, :]

        block = ctx.enter_context(nc.Block())

        @block.sync
        def _(sp):
            row = lambda v: v.rearrange("(a n) -> a n", a=1).to_broadcast([P, v.shape[0]])
            for n, w in enumerate((wq, wk, wv, wo)):
                sp.dma_start(raw_qkvo[:, n], w.rearrange("(c p) n -> p c n", p=P)).then_inc(raw_loaded[0], 16)
            sp.dma_start(x_in[:], x_v[0]).then_inc(x_loaded, 16)
            sp.dma_start(adj_a[:], adj_v[0]).then_inc(adj_a_loaded, 16)
            at = 0
            for v in (ln1_g, ln1_b, ln2_g, ln2_b, bq, bk, bv, b1):
                n = v.shape[0] // P
                sp.dma_start(param_rows[at:at + n, :], v.rearrange("(c p) -> c p", p=P)).then_inc(params_loaded, 16)
                at += n
            for v in (bq1, bk1):
                sp.dma_start(param_rows[at:at + LAYERS, :], v).then_inc(params_loaded, 16)
                at += LAYERS
            assert at == PARAMS
            sp.dma_start(bo_row[:], row(bo)).then_inc(params_loaded, 16)
            sp.dma_start(b2_row[:], row(b2)).then_inc(params_loaded, 16)
            for n in range(LAYERS):
                sp.dma_start(lg_row[:, n], row(ln_g[n])).then_inc(params_loaded, 16)
                sp.dma_start(lb_row[:, n], row(ln_b[n])).then_inc(params_loaded, 16)
            sp.dma_start(raw_1, w1.rearrange("(c p) n -> p c n", p=P)).then_inc(raw_loaded[1], 16)
            sp.dma_start(raw_2, w2.rearrange("(f p) n -> p f n", p=P)).then_inc(raw_loaded[2], 16)
            for n in range(LAYERS):
                sp.dma_start(raw_l[:, n, 0], Wq[n]).then_inc(raw_loaded[3], 16)
                sp.dma_start(raw_l[:, n, 1], Wk[n]).then_inc(raw_loaded[3], 16)
                sp.dma_start(raw_l[:, n, 2:4], Wc[n].rearrange("(c p) d -> p c d", p=P)).then_inc(raw_loaded[3], 16)

            def body(i):
                if on(i - 2):
                    wait(sp, adj_l_used, i - 2)
                    sp.dma_start(adj_l[:], adj_v[i - 2]).then_inc(adj_l_loaded, 16)
                if on(i - 3):
                    wait(sp, l_out, i - 2)
                    sp.dma_start(out_v[i - 3], x3[:]).then_inc(stored, 16)
                if on(i + 1) and (not isinstance(i, int) or i >= 0):
                    wait(sp, x_used, i + 1)
                    sp.dma_start(x_in[:], x_v[i + 1]).then_inc(x_loaded, 16)
                    wait(sp, adj_a_used, i + 1)
                    sp.dma_start(adj_a[:], adj_v[i + 1]).then_inc(adj_a_loaded, 16)

            run(sp, body)
            sp.wait_ge(stored, 16 * GROUPS)

        @block.tensor
        def _(pe):
            def product(dst, lhs, rhs, terms):
                parts = [(a, b) for a, b in ((0, 0), (1, 0), (0, 1))]
                n = len(terms) * len(parts)
                k = 0
                for t in terms:
                    for a, b in parts:
                        last = nc.tensor.matmul(dst, lhs(t, a), rhs(t, b), start=(k == 0), stop=(k == n - 1))
                        k += 1
                return last

            def turn(ring, g, job, src, c):
                dst = wait_empty(pe, ring, g, job)
                for t in range(TILES):
                    last = nc.tensor.transpose(dst[:, t * P:(t + 1) * P], src[:, t, c * P:(c + 1) * P], ident[:])
                last.then_inc(is_filled(ring, job), 1)

            pe.wait_ge(consts, 2)
            pe.wait_ge(raw_loaded[0], 64)
            pe.wait_ge(params_loaded, 16 * 16)
            mm = nc.tensor.matmul
            nc.tensor.transpose(bank[7][:, 0:PARAMS], param_rows, ident[0:PARAMS, 0:PARAMS]).then_inc(prep_p, 1)
            pe.wait_ge(prep_d, 1)
            for n, w in enumerate((0, 1, 2)):
                for o in range(DC):
                    for c in range(DC):
                        last = mm(bank[0][:, 2 * n + o:2 * n + o + 1], raw_qkvo[:, w, c, o * P:(o + 1) * P],
                                  b1c[:, c:c + 1], start=(c == 0), stop=(c == DC - 1))
            pe.wait_ge(raw_loaded[1], 16)
            for f in range(FC):
                for c in range(DC):
                    last = mm(bank[0][:, 8 + f:9 + f], raw_1[:, c, f * P:(f + 1) * P], b2c[:, c:c + 1],
                              start=(c == 0), stop=(c == DC - 1))
            last.then_inc(prep_p, 1)
            pe.wait_ge(prep_d, 2)
            for c in range(DC):
                last = mm(bank[1][:, 0:D], bv_c[:, c:c + 1].to_broadcast([P, P]), raw_qkvo[:, 3, c, :],
                          start=(c == 0), stop=(c == DC - 1))
            last.then_inc(prep_p, 1)
            pe.wait_ge(raw_loaded[3], 96)
            for n in range(LAYERS):
                for w in range(2):
                    for c in range(DC):
                        last = nc.tensor.transpose(bank[2 + n][:, (w * DC + c) * P:(w * DC + c + 1) * P],
                                                   raw_l[:, n, w, c * P:(c + 1) * P], ident[:])
                for c in range(DC):
                    for e in range(DC):
                        last = nc.tensor.transpose(bank[4 + n][:, c * D + e * P:c * D + (e + 1) * P],
                                                   raw_l[:, n, 2 + e, c * P:(c + 1) * P], ident[:])
            last.then_inc(prep_p, 1)
            pe.wait_ge(prep_g, 2)
            pe.wait_ge(prep_d, 5)

            def a_turn(g):
                wait(pe, x_hat_ready, TILES * g + TILES)
                for c in range(DC):
                    turn("A", g, A_JOBS["xT"] + c, x_hat, c)

            def a_qk(g, w):
                for o in range(DC):
                    job = A_JOBS["qk"[w]] + o
                    dst = wait_sources(pe, "A", g, [A_JOBS["xT"], A_JOBS["xT"] + 1], job)
                    product(dst[:], lambda c, s: w_qkv[s][:, w, c, o * P:(o + 1) * P], lambda c, s: xT[s][:, c, :],
                            range(DC)).then_inc(is_filled("A", job), 1)

            def a_v(g):
                for k in range(2):
                    job = A_JOBS["v"] + k
                    dst = wait_empty(pe, "A", g, job)
                    for t in (2 * k, 2 * k + 1):
                        last = product(dst[:, t % 2 * D:(t % 2 + 1) * D], lambda c, s: xT[s][:, c, t * P:(t + 1) * P],
                                       lambda c, s: w_qkv[s][:, 2, c, :], range(DC))
                    last.then_inc(is_filled("A", job), 1)

            def a_scores(g, t):
                job = A_JOBS["s"] + t
                dst = wait_sources(pe, "A", g, range(A_JOBS["q"], A_JOBS["k"] + DC), job)
                for c in range(DC):
                    for b in range(2):
                        n = 2 * t + b
                        last = mm(dst[b * NODES:(b + 1) * NODES, c * 256:(c + 1) * 256],
                                  qT[:, c, n * NODES:(n + 1) * NODES],
                                  kT[:, c, n].rearrange("p j k -> p (j k)"), start=True, stop=True)
                last.then_inc(is_filled("A", job), 1)

            def a_turn_p(g, t):
                wait(pe, p_ready, TILES * g + t + 1)
                job = P_JOB[t]
                dst = wait_empty(pe, "A", g, job)
                for j in range(H0):
                    last = nc.tensor.transpose(dst[:, j * P:(j + 1) * P], sc[:, t, j * P:(j + 1) * P], ident[:])
                last.then_inc(is_filled("A", job), 1)

            H0 = 4

            def a_values(g, k):
                job = O_JOB[k]
                dst = wait_sources(pe, "A", g, [A_JOBS["v"], A_JOBS["v"] + 1, P_JOB[2 * k], P_JOB[2 * k + 1]], job)
                for t in (2 * k, 2 * k + 1):
                    for b in range(2):
                        for j in range(H0):
                            at = (t % 2) * 256 + (j // 2) * P + b * NODES
                            last = mm(dst[j % 2 * 64:j % 2 * 64 + 64, at:at + NODES],
                                      v2[:, 2 * t + b, j].rearrange("p a d -> p (a d)"),
                                      pT[:, t % 2, j * P + b * NODES:j * P + (b + 1) * NODES], start=True, stop=True)
                last.then_inc(is_filled("A", job), 1)

            def a_out(g, k):
                job = A_JOBS["w"] + k
                dst = wait_sources(pe, "A", g, [O_JOB[k]], job)
                for t in (2 * k, 2 * k + 1):
                    last = product(dst[:, t % 2 * D:(t % 2 + 1) * D], lambda c, s: oT[s][:, c, t * P:(t + 1) * P],
                                   lambda c, s: w_o[s][:, c, :], range(DC))
                last.then_inc(is_filled("A", job), 1)

            def h_turn(g):
                wait(pe, x1_hat_ready, TILES * g + TILES)
                for c in range(DC):
                    turn("M", g, M_JOBS["xT"] + c, x1_hat, c)

            def h_up(g, f):
                job = M_JOBS["h"] + f
                dst = wait_sources(pe, "M", g, [M_JOBS["xT"], M_JOBS["xT"] + 1], job)
                product(dst[:], lambda c, s: w_1[s][:, c, f * P:(f + 1) * P], lambda c, s: nT[s][:, c, :],
                        range(DC)).then_inc(is_filled("M", job), 1)

            def y_down(g, k):
                wait(pe, h_lo, FC * g + FC)
                job = M_JOBS["y"] + k
                dst = wait_empty(pe, "M", g, job)
                for t in (2 * k, 2 * k + 1):
                    last = product(dst[:, t % 2 * D:(t % 2 + 1) * D], lambda f, s: hT[s][:, f, t * P:(t + 1) * P],
                                   lambda f, s: w_2[s][:, f, :], range(FC))
                last.then_inc(is_filled("M", job), 1)

            def l_turn(g, l):
                if l == 0:
                    for k in range(2):
                        wait_drained(pe, "M", g, M_JOBS["y"] + k)
                else:
                    wait(pe, l_x, TILES * g + TILES)
                for c in range(DC):
                    turn("L", g, L_JOBS[f"xT{l}"] + c, (x2, x3)[l], c)

            def l_qk(g, l):
                for w in range(2):
                    job = L_JOBS[f"qk{l}"] + w
                    dst = wait_sources(pe, "L", g, [L_JOBS[f"xT{l}"], L_JOBS[f"xT{l}"] + 1], job)
                    product(dst[:], lambda c, s: w_l[s][:, l, w, c, :], lambda c, s: lT[s][:, c, :],
                            range(DC)).then_inc(is_filled("L", job), 1)

            def l_xw(g, l):
                for k in range(2):
                    job = L_JOBS[f"xw{l}"] + k
                    dst = wait_empty(pe, "L", g, job)
                    for t in (2 * k, 2 * k + 1):
                        last = product(dst[:, t % 2 * D:(t % 2 + 1) * D], lambda c, s: lT[s][:, c, t * P:(t + 1) * P],
                                       lambda c, s: w_c[s][:, l, c, :], range(DC))
                    last.then_inc(is_filled("L", job), 1)

            def l_scores(g, l):
                job = L_JOBS[f"s{l}"]
                dst = wait_sources(pe, "L", g, [L_JOBS[f"qk{l}"], L_JOBS[f"qk{l}"] + 1], job)
                for t in range(TILES):
                    at = slice(t * P, (t + 1) * P)
                    last = mm(dst[:, at], lqk[:, 0, at], lqk[:, 1, at], start=True, stop=True)
                last.then_inc(is_filled("L", job), 1)

            def l_turn_p(g, l):
                job = L_JOBS[f"p{l}"]
                dst = wait_empty(pe, "L", g, job)
                for t in range(TILES):
                    wait(pe, l_exp, 2 * TILES * g + TILES * l + t + 1)
                    last = nc.tensor.transpose(dst[:, t * P:(t + 1) * P], ls[:, t], ident[:])
                last.then_inc(is_filled("L", job), 1)

            def l_mix(g, l):
                for k in range(2):
                    job = L_JOBS[f"o{l}"] + k
                    sources = [L_JOBS[f"p{l}"], L_JOBS[f"xw{l}"], L_JOBS[f"xw{l}"] + 1]
                    dst = wait_sources(pe, "L", g, sources, job)
                    for t in (2 * k, 2 * k + 1):
                        last = mm(dst[:, t % 2 * D:(t % 2 + 1) * D], lpT[:, t], lxw[:, t], start=True, stop=True)
                    last.then_inc(is_filled("L", job), 1)

            def body(i):
                if on(i - 3):
                    l_turn_p(i - 3, 1)
                if on(i):
                    a_turn(i)
                if on(i - 3):
                    l_mix(i - 3, 1)
                if on(i):
                    a_qk(i, 0)
                    a_qk(i, 1)
                if on(i - 2):
                    y_down(i - 2, 1)
                if on(i - 1):
                    h_turn(i - 1)
                if on(i):
                    a_v(i)
                    a_scores(i, 0)
                if on(i - 2):
                    l_turn(i - 2, 0)
                if on(i):
                    a_scores(i, 1)
                if on(i - 1):
                    h_up(i - 1, 0)
                if on(i):
                    a_scores(i, 2)
                if on(i - 1):
                    h_up(i - 1, 1)
                    h_up(i - 1, 2)
                if on(i):
                    a_scores(i, 3)
                if on(i - 2):
                    l_qk(i - 2, 0)
                    l_xw(i - 2, 0)
                    l_scores(i - 2, 0)
                if on(i - 1):
                    h_up(i - 1, 3)
                if on(i):
                    a_turn_p(i, 0)
                if on(i - 1):
                    h_up(i - 1, 4)
                if on(i - 2):
                    l_turn_p(i - 2, 0)
                if on(i):
                    a_turn_p(i, 1)
                if on(i - 2):
                    l_mix(i - 2, 0)
                if on(i):
                    a_values(i, 0)
                    a_turn_p(i, 2)
                    a_turn_p(i, 3)
                if on(i - 1):
                    h_up(i - 1, 5)
                    h_up(i - 1, 6)
                if on(i):
                    a_values(i, 1)
                if on(i - 1):
                    h_up(i - 1, 7)
                if on(i - 2):
                    l_turn(i - 2, 1)
                if on(i):
                    a_out(i, 0)
                if on(i - 2):
                    l_qk(i - 2, 1)
                    l_xw(i - 2, 1)
                if on(i):
                    a_out(i, 1)
                if on(i - 2):
                    l_scores(i - 2, 1)
                if on(i - 1):
                    y_down(i - 1, 0)

            run(pe, body)

        @block.scalar
        def _(act):
            act.wait_ge(prep_d, 5)
            act.wait_ge(prep_p, 4)
            act.wait_ge(prep_g, 2)

            def a_hi(g):
                for c in range(DC):
                    src = wait_filled(act, "A", g, A_JOBS["xT"] + c)
                    nc.scalar.activation(xT[0][:, c], src[:], ACT.Identity).then_inc(hi_a, 1)

            def a_qk(g):
                for c in range(DC):
                    job = A_JOBS["q"] + c
                    src = wait_filled(act, "A", g, job)
                    nc.scalar.activation(qT[:, c], src[:], ACT.Identity, bias=bq_c[:, c:c + 1],
                                         scale=SCALE0).then_inc(is_drained("A", job), 1)
                for c in range(DC):
                    job = A_JOBS["k"] + c
                    src = wait_filled(act, "A", g, job)
                    for j in range(QUADS):
                        at = slice(j * HD, (j + 1) * HD)
                        last = nc.scalar.activation(kT[at, c, :, j, :], src[at, :].rearrange("p (g k) -> p g k", k=NODES),
                                                    ACT.Identity, bias=bk_c[at, c:c + 1])
                    last.then_inc(is_drained("A", job), 1)

            def a_v(g):
                for k in range(2):
                    job = A_JOBS["v"] + k
                    src = wait_filled(act, "A", g, job)[:].rearrange("p (t j a d) -> p t j a d", t=2, a=2, d=HD)
                    for b in range(2):
                        for a in range(2):
                            dst = v2[a * 64:(a + 1) * 64].rearrange("p (t b) j a d -> p t b j a d", b=2)
                            last = nc.scalar.activation(dst[:, 2 * k:2 * k + 2, b, :, a, :],
                                                        src[b * 64:(b + 1) * 64, :, :, a, :], ACT.Identity)
                    last.then_inc(is_drained("A", job), 1)

            def a_exp(g, t):
                wait(act, shifted, TILES * g + t + 1)
                nc.scalar.activation(sc[:, t], sc[:, t], ACT.Exp).then_inc(exp_done, 1)

            def a_copy_p(g, t):
                src = wait_filled(act, "A", g, P_JOB[t])
                nc.scalar.activation(pT[:, t % 2], src[:], ACT.Identity).then_inc(is_drained("A", P_JOB[t]), 1)

            def a_hi_o(g, k):
                src = wait_filled(act, "A", g, O_JOB[k])[:].rearrange("p (t c r) -> p t c r", t=2, c=DC)
                dst = oT[0][:].rearrange("p c (t r) -> p t c r", r=P)[:, 2 * k:2 * k + 2]
                nc.scalar.activation(dst, src, ACT.Identity).then_inc(hi_a, 1)

            def h_hi_x(g):
                for c in range(DC):
                    src = wait_filled(act, "M", g, M_JOBS["xT"] + c)
                    nc.scalar.activation(nT[0][:, c], src[:], ACT.Identity).then_inc(hi_m, 1)

            def h_gelu(g, f):
                wait(act, h_lo, FC * g + max(f - HB + 1, 0))
                job = M_JOBS["h"] + f
                src = wait_filled(act, "M", g, job)
                nc.scalar.activation(hf[:, f % HB], src[:], ACT.Gelu, bias=bh_c[:, f:f + 1])
                nc.scalar.activation(hT[0][:, f], src[:], ACT.Gelu, bias=bh_c[:, f:f + 1])\
                    .then_inc(is_drained("M", job), 1)

            def l_hi(g, l):
                for c in range(DC):
                    src = wait_filled(act, "L", g, L_JOBS[f"xT{l}"] + c)
                    nc.scalar.activation(lT[0][:, c], src[:], ACT.Identity).then_inc(hi_l, 1)

            def l_copies(g, l):
                for w in range(2):
                    job = L_JOBS[f"qk{l}"] + w
                    src = wait_filled(act, "L", g, job)
                    nc.scalar.activation(lqk[:, w], src[:], ACT.Identity, bias=(lq_c, lk_c)[w][:, l:l + 1],
                                         scale=(SCALE1, 1.0)[w]).then_inc(is_drained("L", job), 1)
                for k in range(2):
                    job = L_JOBS[f"xw{l}"] + k
                    src = wait_filled(act, "L", g, job)
                    nc.scalar.activation(lxw[:, 2 * k:2 * k + 2].rearrange("p t d -> p (t d)"), src[:], ACT.Identity)\
                        .then_inc(is_drained("L", job), 1)

            def l_exps(g, l):
                wait(act, l_top, 2 * g + l + 1)
                for t in range(TILES):
                    nc.scalar.activation(ls[:, t], ls[:, t], ACT.Exp, bias=ltop[:, t:t + 1],
                                         accum_out=lsum[:, t:t + 1]).then_inc(l_exp, 1)

            def l_copy_p(g, l):
                job = L_JOBS[f"p{l}"]
                src = wait_filled(act, "L", g, job)
                nc.scalar.activation(lqk[:, 0, :], src[:], ACT.Identity)\
                    .then_inc(is_drained("L", job), 1)

            def body(i):
                if on(i - 3):
                    l_copy_p(i - 3, 1)
                if on(i):
                    a_hi(i)
                    a_qk(i)
                if on(i - 1):
                    h_hi_x(i - 1)
                if on(i):
                    a_v(i)
                if on(i - 2):
                    l_hi(i - 2, 0)
                if on(i):
                    a_exp(i, 0)
                if on(i - 1):
                    h_gelu(i - 1, 0)
                    h_gelu(i - 1, 1)
                    h_gelu(i - 1, 2)
                if on(i):
                    a_exp(i, 1)
                if on(i - 2):
                    l_copies(i - 2, 0)
                if on(i):
                    a_exp(i, 2)
                    a_exp(i, 3)
                if on(i - 2):
                    l_exps(i - 2, 0)
                    l_copy_p(i - 2, 0)
                if on(i):
                    a_copy_p(i, 0)
                    a_copy_p(i, 1)
                if on(i - 1):
                    h_gelu(i - 1, 3)
                    h_gelu(i - 1, 4)
                if on(i):
                    a_copy_p(i, 2)
                    a_hi_o(i, 0)
                    a_copy_p(i, 3)
                if on(i - 1):
                    h_gelu(i - 1, 5)
                if on(i - 2):
                    l_hi(i - 2, 1)
                if on(i - 1):
                    h_gelu(i - 1, 6)
                if on(i):
                    a_hi_o(i, 1)
                if on(i - 1):
                    h_gelu(i - 1, 7)
                if on(i - 2):
                    l_copies(i - 2, 1)
                    l_exps(i - 2, 1)

            run(act, body)

        @block.gpsimd
        def _(pool):
            nc.gpsimd.memset(ident[:], 0.0).then_inc(consts, 1)
            pool.wait_ge(consts, 1)
            nc.gpsimd.affine_select(out=ident[:], in_=ident[:], compare_op=ALU.not_equal, fill=1.0, base=0,
                                    pattern=[[-1, P]], channel_multiplier=1).then_inc(consts, 1)
            nc.gpsimd.memset(minus_half, -0.5)
            nc.gpsimd.memset(pen1[:], MASKED)
            pool.wait_ge(prep_d, 5)
            pool.wait_ge(prep_p, 4)
            nc.gpsimd.memset(kT[:], 0.0).then_inc(prep_g, 1)
            nc.gpsimd.memset(v2[:], 0.0).then_inc(prep_g, 1)
            pool.wait_ge(prep_g, 2)

            def normalise(g, s, src, dst, chain, ready):
                _, _, nm, ve, rs = stats[s]
                wait(pool, {"A": stats_a, "H": stats_h}[s], 2 * g + 2)
                nc.gpsimd.tensor_tensor(rs[:], ve[:], minus_half, ALU.pow).then_inc(chain, 1)
                wait(pool, chain, g + 1)
                nc.gpsimd.tensor_tensor(spare_p, minus_half[:, 0:1], minus_half[:, 0:1], ALU.add)
                for t in range(TILES):
                    nc.gpsimd.tensor_scalar(dst[:, t], src[:, t], nm[:, t:t + 1], rs[:, t:t + 1], ALU.add,
                                            ALU.mult).then_inc(ready, 1)

            def a_normalise(g):
                normalise(g, "A", x_in, x_hat, pool_a, x_hat_ready)

            def a_add_bo(g):
                wait(pool, x1_b2_ready, g)
                wait(pool, x1_hat_ready, TILES * g)
                nc.gpsimd.tensor_tensor(x1[:], x_in[:], bo_row[:].rearrange("p (t d) -> p t d", t=1)
                                        .to_broadcast([P, TILES, D]), ALU.add).then_inc(x1_begun, 1)
                wait(pool, x1_begun, g + 1)
                pool.sem_inc(x_used, 1)

            def h_normalise(g):
                if on(g + 1):
                    for c in range(DC):
                        wait_filled(pool, "A", g + 1, A_JOBS["xT"] + c)
                normalise(g, "H", x1, x1_hat, pool_h, x1_hat_ready)

            def h_add_b2(g):
                for k in range(2):
                    wait_all_drained_before(pool, "M", g, M_JOBS["y"] + k)
                nc.gpsimd.tensor_tensor(x1_b2[:], x1[:], b2_row[:].rearrange("p (t d) -> p t d", t=1)
                                        .to_broadcast([P, TILES, D]), ALU.add).then_inc(x1_b2_ready, 1)

            def l_rstd(g, l):
                _, _, nm, ve, rs = stats["L"]
                wait(pool, stats_l, 2 * (2 * g + l + 1))
                nc.gpsimd.tensor_tensor(rs[:], ve[:], minus_half, ALU.pow).then_inc(rstd_l, 1)

            def body(i):
                if on(i - 3):
                    l_rstd(i - 3, 1)
                if on(i - 1):
                    h_normalise(i - 1)
                    h_add_b2(i - 1)
                if on(i - 2):
                    l_rstd(i - 2, 0)
                if on(i):
                    a_add_bo(i)
                if on(i + 1):
                    a_normalise(i + 1)

            run(pool, body)

        @block.vector
        def _(dve):
            tt = nc.vector.tensor_tensor
            ts = nc.vector.tensor_scalar
            stt = nc.vector.scalar_tensor_tensor
            dve.wait_ge(params_loaded, 16 * 16)
            dve.wait_ge(prep_p, 1)
            nc.vector.tensor_copy(cols[:, 0:PARAMS], bank[7][:, 0:PARAMS]).then_inc(prep_d, 1)
            dve.wait_ge(prep_d, 1)
            dve.wait_ge(prep_p, 2)
            tt(cols[:, 8:14], cols[:, 8:14], bank[0][:, 0:6], ALU.add)
            tt(bh_c, bh_c, bank[0][:, 8:16], ALU.add).then_inc(prep_d, 1)
            dve.wait_ge(prep_d, 2)
            ts(bq_c, bq_c, SCALE0, None, ALU.mult)
            ts(lq_c, lq_c, SCALE1, None, ALU.mult)
            dve.wait_ge(prep_p, 3)
            tt(bo_row[:], bo_row[:], bank[1][:, 0:D], ALU.add).then_inc(prep_d, 1)
            dve.wait_ge(raw_loaded[1], 16)
            dve.wait_ge(raw_loaded[2], 16)
            for c in range(DC):
                ts(raw_qkvo[:, 0:3, c], raw_qkvo[:, 0:3, c], g1c[:, c:c + 1], None, ALU.mult)
                ts(raw_1[:, c], raw_1[:, c], g2c[:, c:c + 1], None, ALU.mult).then_inc(prep_a, 1)
            dve.wait_ge(prep_a, 2)
            dve.wait_ge(prep_p, 4)
            pairs = [(raw_qkvo[:, 0:3], w_qkv, slice(None)), (raw_qkvo[:, 3], w_o, slice(None)),
                     (raw_1, w_1, slice(None)), (raw_2, w_2, slice(None))]
            for n in range(LAYERS):
                pairs.append((bank[2 + n][:].rearrange("p (w c f) -> p w c f", w=2, c=DC),
                              (w_l[0][:, n], w_l[1][:, n]), None))
                pairs.append((bank[4 + n][:].rearrange("p (c d) -> p c d", c=DC), (w_c[0][:, n], w_c[1][:, n]), None))
            views = [(src, parts[0] if at is None else parts[0][:], parts[1] if at is None else parts[1][:])
                     for src, parts, at in pairs]
            for src, hi, lo in views:
                last = nc.vector.tensor_copy(hi, src)
            last.then_inc(prep_d, 1)
            dve.wait_ge(prep_d, 4)
            for src, hi, lo in views:
                last = tt(lo, src, hi.bitcast(F32), ALU.subtract)
            last.then_inc(prep_d, 1)

            class Chain:

                def __init__(self, s, per_group, g, n=0):
                    self.s, self.base, self.n = s, g * per_group, n

                def step(self, ins):
                    self.n += 1
                    ins.then_inc(self.s, 1)

                def wait(self):
                    wait(dve, self.s, self.base + self.n)

            def norm_stats(s, src, chain, ready):
                st, mv, nm, ve, rs = stats[s]
                for t in range(TILES):
                    ins = nc.vector.bn_stats(st[:, t], src[:, t])
                chain.step(ins)
                chain.wait()
                nc.vector.memset(spare_d, 0.0)
                for t in range(TILES):
                    ins = nc.vector.bn_aggr(mv[:, t], st[:, t])
                chain.step(ins)
                chain.wait()
                ts(nm[:], mv[:, :, 0], -1.0, None, ALU.mult).then_inc(ready, 1)
                ts(ve[:], mv[:, :, 1], EPS, None, ALU.add).then_inc(ready, 1)

            N_STEPS = 2
            A_STEPS = 1 + 3 * TILES
            H_STEPS = 2
            L_STEPS = LAYERS * 4

            def a_norm(g, ch):
                wait(dve, x_loaded, 16 * g + 16)
                norm_stats("A", x_in, ch, stats_a)

            def a_edges(g, ch):
                wait(dve, adj_a_loaded, 16 * g + 16)
                stt(bias0[:], adj_a[:], 0.1, adj_a[:], ALU.mult, ALU.mult)
                ts(pen[:], adj_a[:], 0, MASKED, ALU.is_le, ALU.mult).then_inc(adj_a_used, 1)
                wait(dve, adj_a_used, g + 1)
                ch.step(tt(bias0[:], bias0[:], pen[:], ALU.add))

            def lo_of(ring, g, job, hi_sem, count, hi, lo, view=None):
                src = wait_filled(dve, ring, g, job)[:]
                if view:
                    src = view(src)
                wait(dve, hi_sem, count)
                tt(lo, src, hi.bitcast(F32), ALU.subtract).then_inc(is_drained(ring, job), 1)

            def a_lo(g):
                for c in range(DC):
                    lo_of("A", g, A_JOBS["xT"] + c, hi_a, 4 * g + c + 1, xT[0][:, c], xT[1][:, c])

            heads = lambda a: a.rearrange("p (h k) -> p h k", h=H)
            spread = lambda a: a.rearrange("p (h k) -> p h k", k=1).to_broadcast([P, H, NODES])

            def a_front(g, t, ch):
                job = A_JOBS["s"] + t
                src = wait_filled(dve, "A", g, job)
                s = heads(sc[:, t])
                if t == 0:
                    ch.wait()
                tt(s, heads(src[:]), bias0[:, t].rearrange("p (h k) -> p h k", h=1).to_broadcast([P, H, NODES]),
                   ALU.add).then_inc(is_drained("A", job), 1)
                wait_drained(dve, "A", g, job)
                ch.step(nc.vector.reduce_max(top[:, t], s, AX_X))
                ch.wait()
                tt(s, s, spread(top[:, t]), ALU.subtract).then_inc(shifted, 1)

            def a_back(g, t, ch):
                wait(dve, exp_done, TILES * g + t + 1)
                e = heads(sc[:, t])
                ch.step(nc.vector.reduce_sum(total[:, t], e, AX_X))
                ch.wait()
                ch.step(nc.vector.reciprocal(share[:, t], total[:, t]))
                ch.wait()
                tt(heads(sc[:, t]), e, spread(share[:, t]), ALU.mult).then_inc(p_ready, 1)

            def a_lo_o(g, k):
                dst = [oT[s][:].rearrange("p c (t r) -> p t c r", r=P)[:, 2 * k:2 * k + 2] for s in range(2)]
                lo_of("A", g, O_JOB[k], hi_a, 4 * g + 3 + k, dst[0], dst[1],
                      lambda b: b.rearrange("p (t c r) -> p t c r", t=2, c=DC))

            def a_residual(g, k):
                if k == 0:
                    wait(dve, x1_begun, g + 1)
                job = A_JOBS["w"] + k
                src = wait_filled(dve, "A", g, job)
                tt(x1[:, 2 * k:2 * k + 2], src[:].rearrange("p (t d) -> p t d", t=2), x1[:, 2 * k:2 * k + 2],
                   ALU.add).then_inc(is_drained("A", job), 1)

            def h_norm(g, ch):
                for k in range(2):
                    wait_drained(dve, "A", g, A_JOBS["w"] + k)
                norm_stats("H", x1, ch, stats_h)

            def h_lo_x(g):
                for c in range(DC):
                    lo_of("M", g, M_JOBS["xT"] + c, hi_m, DC * g + c + 1, nT[0][:, c], nT[1][:, c])

            def h_rest(g, f):
                wait_drained(dve, "M", g, M_JOBS["h"] + f)
                tt(hT[1][:, f], hf[:, f % HB], hT[0][:, f].bitcast(F32), ALU.subtract).then_inc(h_lo, 1)

            def y_residual(g, k):
                if k == 0:
                    wait(dve, x1_b2_ready, g + 1)
                job = M_JOBS["y"] + k
                src = wait_filled(dve, "M", g, job)
                tt(x2[:, 2 * k:2 * k + 2], src[:].rearrange("p (t d) -> p t d", t=2), x1_b2[:, 2 * k:2 * k + 2],
                   ALU.add).then_inc(is_drained("M", job), 1)

            def l_mask(g):
                wait(dve, adj_l_loaded, 16 * g + 16)
                for b in range(2):
                    at = slice(b * NODES, (b + 1) * NODES)
                    ins = ts(pen1[at, :, b, :], adj_l[at], 0, MASKED, ALU.is_equal, ALU.mult)
                ins.then_inc(adj_l_used, 1)
                wait(dve, adj_l_used, g + 1)

            def l_lo(g, l):
                for c in range(DC):
                    lo_of("L", g, L_JOBS[f"xT{l}"] + c, hi_l, 2 * DC * g + DC * l + c + 1, lT[0][:, c], lT[1][:, c])

            def l_front(g, l, ch):
                job = L_JOBS[f"s{l}"]
                src = wait_filled(dve, "L", g, job)
                tt(ls[:].rearrange("p t n -> p (t n)"), src[:], pen1[:].rearrange("p t b k -> p (t b k)"),
                   ALU.add).then_inc(is_drained("L", job), 1)
                wait_drained(dve, "L", g, job)
                nc.vector.tensor_reduce(ltop[:], ls[:], AX_X, ALU.max, negate=True).then_inc(l_top, 1)

            def l_mix(g, l, ch):
                wait(dve, l_exp, 2 * TILES * g + TILES * (l + 1))
                ch.step(nc.vector.reciprocal(lshare[:], lsum[:]))
                ch.wait()
                prev = (x2, x3)[l]
                if l == 0:
                    for k in range(2):
                        wait_drained(dve, "M", g, M_JOBS["y"] + k)
                for t in range(TILES):
                    job = L_JOBS[f"o{l}"] + t // 2
                    src = wait_filled(dve, "L", g, job) if t % 2 == 0 else src
                    ins = stt(prev[:, t], src[:, t % 2 * D:(t % 2 + 1) * D], lshare[:, t:t + 1], prev[:, t], ALU.mult,
                              ALU.add)
                    if t % 2:
                        ins.then_inc(is_drained("L", job), 1)
                for k in range(2):
                    wait_drained(dve, "L", g, L_JOBS[f"o{l}"] + k)
                norm_stats("L", prev, ch, stats_l)

            def l_norm(g, l, ch):
                prev = (x2, x3)[l]
                _, _, nm, ve, rs = stats["L"]
                wait(dve, stats_l, 2 * (2 * g + l + 1))
                for t in range(TILES):
                    ins = stt(prev[:, t], prev[:, t], nm[:, t:t + 1], lg_row[:, l], ALU.add, ALU.mult)
                ch.step(ins)
                wait(dve, rstd_l, 2 * g + l + 1)
                ch.wait()
                if l == 0:
                    wait(dve, stored, 16 * g)
                for t in range(TILES):
                    ins = stt(x3[:, t], prev[:, t], rs[:, t:t + 1], lb_row[:, l], ALU.mult, ALU.add)
                    if l == 0:
                        ins.then_inc(l_x, 1)
                if l == 1:
                    ins.then_inc(l_out, 1)
                else:
                    wait(dve, l_x, TILES * g + TILES)

            def body(i):
                ca = Chain(dve_a, A_STEPS, i)
                cn = Chain(dve_n, N_STEPS, i + 1)
                chh = Chain(dve_h, H_STEPS, i - 1)
                cl = Chain(dve_l, L_STEPS, i - 2)
                ct = Chain(dve_l, L_STEPS, i - 3, L_STEPS // 2)
                if on(i - 1):
                    h_norm(i - 1, chh)
                if on(i):
                    a_lo(i)
                if on(i - 3):
                    l_mix(i - 3, 1, ct)
                if on(i):
                    a_edges(i, ca)
                if on(i - 2):
                    y_residual(i - 2, 0)
                if on(i - 3):
                    l_norm(i - 3, 1, ct)
                if on(i - 2):
                    y_residual(i - 2, 1)
                if on(i - 1):
                    h_lo_x(i - 1)
                if on(i - 2):
                    l_mask(i - 2)
                if on(i):
                    a_front(i, 0, ca)
                    a_front(i, 1, ca)
                if on(i - 2):
                    l_lo(i - 2, 0)
                if on(i - 1):
                    h_rest(i - 1, 0)
                if on(i):
                    a_front(i, 2, ca)
                if on(i - 1):
                    h_rest(i - 1, 1)
                if on(i):
                    a_back(i, 0, ca)
                    a_back(i, 1, ca)
                    a_front(i, 3, ca)
                if on(i - 2):
                    l_front(i - 2, 0, cl)
                if on(i):
                    a_back(i, 2, ca)
                    a_back(i, 3, ca)
                if on(i - 1):
                    h_rest(i - 1, 2)
                if on(i - 2):
                    l_mix(i - 2, 0, cl)
                if on(i - 1):
                    h_rest(i - 1, 3)
                if on(i - 2):
                    l_norm(i - 2, 0, cl)
                if on(i):
                    a_lo_o(i, 0)
                if on(i - 1):
                    h_rest(i - 1, 4)
                if on(i - 2):
                    l_lo(i - 2, 1)
                if on(i - 1):
                    h_rest(i - 1, 5)
                if on(i):
                    a_lo_o(i, 1)
                if on(i - 1):
                    h_rest(i - 1, 6)
                if on(i + 1):
                    a_norm(i + 1, cn)
                if on(i - 1):
                    h_rest(i - 1, 7)
                if on(i):
                    a_residual(i, 0)
                if on(i - 2):
                    l_front(i - 2, 1, cl)
                if on(i):
                    a_residual(i, 1)
                assert not on(i) or ca.n == A_STEPS
                assert not on(i + 1) or cn.n == N_STEPS
                assert not on(i - 1) or chh.n == H_STEPS
                assert not on(i - 2) or cl.n == L_STEPS // 2
                assert not on(i - 3) or ct.n == L_STEPS

            run(dve, body)


_INS = ['x', 'adj', 'L0_gnn_ln1_g', 'L0_gnn_ln1_b', 'L0_gnn_ln2_g', 'L0_gnn_ln2_b', 'L0_gnn_wq', 'L0_gnn_bq',
        'L0_gnn_wk', 'L0_gnn_bk', 'L0_gnn_wv', 'L0_gnn_bv', 'L0_gnn_wo', 'L0_gnn_bo', 'L0_gnn_w1', 'L0_gnn_b1',
        'L0_gnn_w2', 'L0_gnn_b2', 'L1_gnn_Wq', 'L1_gnn_bq', 'L1_gnn_Wk', 'L1_gnn_bk', 'L1_gnn_Wc', 'L1_gnn_ln_g',
        'L1_gnn_ln_b']


def kernel(**inputs):
    import numpy as _np
    import concourse.bacc as _bacc
    from concourse import mybir as _mybir
    from concourse.bass_utils import run_bass_kernel_spmd as _run

    nc = _bacc.Bacc("TRN2", target_bir_lowering=False, num_devices=1)
    arrays, args = {}, []
    for name in _INS:
        a = _np.ascontiguousarray(inputs[name])
        arrays[f"in_{name}_dram"] = a
        args.append(nc.dram_tensor(f"in_{name}_dram", a.shape, _mybir.dt.from_np(a.dtype), kind="ExternalInput").ap())
    shape = arrays["in_x_dram"].shape
    args.append(nc.dram_tensor("out_0_dram", shape, _mybir.dt.float32, kind="ExternalOutput").ap())
    gnn_kernel(nc, *args)
    r = _run(nc, [arrays], core_ids=[0])
    return r.results[0]["out_0_dram"]
```

```python
from contextlib import ExitStack

import concourse.bass as bass
from concourse import mybir

P = 128
TILES = 4
ROWS = TILES * P
NODES = 64
GRAPHS = ROWS // NODES
EPS = 1e-5
MASKED = -1e30

ALU = mybir.AluOpType
ACT = mybir.ActivationFunctionType
F32 = mybir.dt.float32
F32R = mybir.dt.float32r
I32 = mybir.dt.int32
AX_X = mybir.AxisListType.X


def number(jobs):
    first, n = {}, 0
    for name, count in jobs:
        first[name] = n
        n += count
    return first, n


A_JOBS, A_COUNT = number([("xT", 2), ("q", 2), ("k", 2), ("v", 2), ("s", 4), ("p01", 2), ("o01", 1),
                          ("p23", 2), ("o23", 1), ("w", 2)])
M_JOBS, M_COUNT = number([("xT", 2), ("h", 8), ("y", 2)])
L_JOBS, L_COUNT = number([(f"{name}{layer}", count) for layer in range(2)
                          for name, count in (("xT", 2), ("qk", 2), ("xw", 2), ("s", 1), ("p", 1), ("o", 2))])
RING = {"A": 4, "M": 2, "L": 2}
COUNT = {"A": A_COUNT, "M": M_COUNT, "L": L_COUNT}
BASE = {"A": 0, "M": 4, "L": 6}
assert all(COUNT[s] % RING[s] == 0 for s in RING)
P_JOB = [A_JOBS["p01"], A_JOBS["p01"] + 1, A_JOBS["p23"], A_JOBS["p23"] + 1]
O_JOB = [A_JOBS["o01"], A_JOBS["o23"]]


def gnn_kernel(nc, x, adj, ln1_g, ln1_b, ln2_g, ln2_b, wq, bq, wk, bk, wv, bv, wo, bo, w1, b1, w2, b2,
               Wq, bq1, Wk, bk1, Wc, ln_g, ln_b, out):
    B, S, D = x.shape
    F = w1.shape[1]
    FF = Wq.shape[1]
    DC = D // P
    FC = F // P
    H = 8
    HD = D // H
    QUADS = P // HD
    GROUPS = B * S // ROWS
    LAYERS = Wq.shape[0]
    assert S == NODES and D == 256 and HD == 32 and FF == P and LAYERS == 2 and H * NODES == 512
    SCALE0 = float(HD) ** -0.5
    SCALE1 = float(FF) ** -0.5

    x_v = x.rearrange("(G t b) s d -> G (b s) t d", t=TILES, b=2)
    adj_v = adj.rearrange("(G t b) s k -> G (b s) t k", t=TILES, b=2)
    out_v = out.rearrange("(G t b) s d -> G (b s) t d", t=TILES, b=2)

    with ExitStack() as ctx:
        def sb(name, shape, dt=F32):
            return ctx.enter_context(nc.sbuf_tensor(name, shape, dt))

        def sem(name):
            return ctx.enter_context(nc.semaphore(name))

        def split(name, shape):
            return sb(name + "_hi", shape, F32R), sb(name + "_lo", shape, F32R)

        bank = [ctx.enter_context(nc.psum_tensor(f"bank{n}", [P, 512], F32)) for n in range(8)]
        filled = [sem(f"filled{n}") for n in range(8)]
        drained = [sem(f"drained{n}") for n in range(8)]

        w_qkv = split("w_qkv", [P, 3, DC, D])
        w_o = split("w_o", [P, DC, D])
        w_1 = split("w_1", [P, DC, F])
        w_2 = split("w_2", [P, FC, D])
        w_l = split("w_l", [P, LAYERS, 2, DC, FF])
        w_c = split("w_c", [P, LAYERS, DC, D])
        shared = sb("shared", [P, 6, TILES * D])
        raw_qkvo = shared[:, 0:2].rearrange("p a (b c n) -> p (a b) c n", b=2, c=DC)
        raw_l = shared[:, 0:2].rearrange("p l (w e) -> p l w e", w=4)
        raw_1 = shared[:, 2:4]
        raw_2 = shared[:, 4:6].rearrange("p a (f n) -> p (a f) n", n=D)
        ident = sb("ident", [P, P])
        cols = sb("cols", [P, 32])
        g1c, b1c, bq_c, bk_c, bv_c, g2c, b2c = (cols[:, 2 * n:2 * n + 2] for n in range(7))
        bh_c = cols[:, 14:22]
        lq_c, lk_c = cols[:, 22:24], cols[:, 24:26]
        bo_row = sb("bo_row", [P, D])
        b2_row = sb("b2_row", [P, D])
        lg_row = sb("lg_row", [P, LAYERS, D])
        lb_row = sb("lb_row", [P, LAYERS, D])
        spare_d, spare_p = cols[:, 26:27], cols[:, 27:28]
        minus_half = cols[:, 28:32]

        x_in = sb("x_in", [P, TILES, D])
        adj_a = sb("adj_a", [P, TILES, NODES], I32)
        pen = sb("pen", [P, TILES, NODES])
        bias0 = sb("bias0", [P, TILES, NODES])
        x_hat = sb("x_hat", [P, TILES, D])
        xT = split("xT", [P, DC, ROWS])
        qT = sb("qT", [P, DC, ROWS])
        kT = sb("kT", [P, DC, GRAPHS, QUADS, NODES])
        v2 = sb("v2", [P, GRAPHS, H // 2, 2, HD])
        top = sb("top", [P, TILES, H])
        total = sb("total", [P, TILES, H])
        share = sb("share", [P, TILES, H])
        sc = sb("sc", [P, TILES, 512])
        pT = qT
        oT = xT
        x1 = sb("x1", [P, TILES, D])
        x1_hat = x_hat
        x1_b2 = shared[:, 4].rearrange("p (t d) -> p t d", t=TILES)
        nT = split("nT", [P, DC, ROWS])
        HB = 2
        hf = shared[:, 5].rearrange("p (b r) -> p b r", b=HB)
        hT = split("hT", [P, FC, ROWS])
        x2 = shared[:, 0].rearrange("p (t d) -> p t d", t=TILES)
        adj_l = sb("adj_l", [P, TILES, NODES], I32)
        pen1 = sb("pen1", [P, TILES, NODES])
        lT = split("lT", [P, DC, ROWS])
        lqk = shared[:, 2].rearrange("p (w r) -> p w r", w=2)
        lxw = shared[:, 3].rearrange("p (t d) -> p t d", t=TILES)
        ls = sb("ls", [P, TILES, NODES])
        le = sb("le", [P, TILES, P])
        lpT = lqk[:, 0, :].rearrange("p (t n) -> p t n", t=TILES)
        ltop = sb("ltop", [P, TILES])
        lsum = sb("lsum", [P, TILES])
        lshare = sb("lshare", [P, TILES])
        x3 = shared[:, 1].rearrange("p (t d) -> p t d", t=TILES)
        stats = {s: (sb(f"st_{s}", [P, TILES, 6]), sb(f"mv_{s}", [P, TILES, 2]), sb(f"nm_{s}", [P, TILES]),
                     sb(f"ve_{s}", [P, TILES]), sb(f"rs_{s}", [P, TILES])) for s in "AHL"}

        params_loaded, more_params_loaded = sem("params_loaded"), sem("more_params_loaded")
        bo_loaded, rows_loaded = sem("bo_loaded"), sem("rows_loaded")
        qkvo_loaded, raw_1_loaded, raw_2_loaded = sem("qkvo_loaded"), sem("raw_1_loaded"), sem("raw_2_loaded")
        raw_l_loaded = sem("raw_l_loaded")
        consts = sem("consts")
        prep_d = sem("prep_d")
        prep_p = sem("prep_p")
        zeroed = sem("zeroed")
        hi_w, lo_w = sem("hi_w"), sem("lo_w")
        x_loaded = sem("x_loaded")
        x_used = sem("x_used")
        adj_a_loaded = sem("adj_a_loaded")
        adj_a_used = sem("adj_a_used")
        adj_l_loaded = sem("adj_l_loaded")
        adj_l_used = sem("adj_l_used")
        stored = sem("stored")
        dve_n, dve_a, dve_h, dve_l = sem("dve_n"), sem("dve_a"), sem("dve_h"), sem("dve_l")
        pool_a, pool_h = sem("pool_a"), sem("pool_h")
        stats_a, stats_h, stats_l = sem("stats_a"), sem("stats_h"), sem("stats_l")
        rstd_l = sem("rstd_l")
        x_hat_ready, x1_hat_ready = sem("x_hat_ready"), sem("x1_hat_ready")
        x1_begun, x1_b2_ready = sem("x1_begun"), sem("x1_b2_ready")
        hi_a, hi_m, hi_l = sem("hi_a"), sem("hi_m"), sem("hi_l")
        shifted, exp_done, p_ready = sem("shifted"), sem("exp_done"), sem("p_ready")
        h_lo = sem("h_lo")
        l_top, l_exp, l_x, l_out = sem("l_top"), sem("l_exp"), sem("l_x"), sem("l_out")

        def wait(eng, s, value):
            if not isinstance(value, int) or value > 0:
                eng.wait_ge(s, value)

        def wait_filled(eng, ring, g, job):
            n = BASE[ring] + job % RING[ring]
            wait(eng, filled[n], g * (COUNT[ring] // RING[ring]) + job // RING[ring] + 1)
            return bank[n]

        def wait_drained(eng, ring, g, job):
            wait(eng, drained[BASE[ring] + job % RING[ring]], g * (COUNT[ring] // RING[ring]) + job // RING[ring] + 1)

        def wait_sources(eng, ring, g, sources, job):
            uses = {job % RING[ring]: job // RING[ring]}
            for n in sources:
                uses[n % RING[ring]] = max(uses.get(n % RING[ring], 0), n // RING[ring] + 1)
            for n, count in uses.items():
                wait(eng, drained[BASE[ring] + n], g * (COUNT[ring] // RING[ring]) + count)
            return bank[BASE[ring] + job % RING[ring]]

        def wait_drained_before(eng, ring, g, job):
            wait(eng, drained[BASE[ring] + job % RING[ring]], g * (COUNT[ring] // RING[ring])
                 - (COUNT[ring] - 1 - job) // RING[ring])

        def wait_empty(eng, ring, g, job):
            n = BASE[ring] + job % RING[ring]
            wait(eng, drained[n], g * (COUNT[ring] // RING[ring]) + job // RING[ring])
            return bank[n]

        def is_filled(ring, job):
            return filled[BASE[ring] + job % RING[ring]]

        def is_drained(ring, job):
            return drained[BASE[ring] + job % RING[ring]]

        def on(g):
            return not isinstance(g, int) or 0 <= g < GROUPS

        def run(eng, body, prepare=lambda i: None):
            for i in range(-1, 3):
                prepare(i)
                body(i)
            with eng.Fori(3, GROUPS - 1) as i:
                body(i)
            for i in range(GROUPS - 1, GROUPS + 3):
                body(i)

        PARAMS = (10, 16)
        param_rows = [sc[0:n, k, 0:P] for k, n in enumerate(PARAMS)]

        PARAM_LOADS, ROW_LOADS = 5, 1 + 2 * LAYERS

        def turned_weights(n):
            return [(bank[4 + n][:].rearrange("p (w c f) -> p w c f", w=2, c=DC), w_l[0][:, n], w_l[1][:, n]),
                    (bank[6 + n][:].rearrange("p (c d) -> p c d", c=DC), w_c[0][:, n], w_c[1][:, n])]

        block = ctx.enter_context(nc.Block())

        @block.sync
        def _(sp):
            def load_params(batch, vectors, loaded):
                at = 0
                for v in vectors:
                    n = v.shape[0] // P if len(v.shape) == 1 else v.shape[0]
                    src = v.rearrange("(c p) -> c p", p=P) if len(v.shape) == 1 else v
                    sp.dma_start(param_rows[batch][at:at + n, :], src).then_inc(loaded, 16)
                    at += n
                assert at == PARAMS[batch]

            load_params(0, (ln1_g, ln1_b, bq, bk, bv), params_loaded)
            sp.dma_start(x_in[:], x_v[0]).then_inc(x_loaded, 16)
            load_params(1, (ln2_g, ln2_b, b1, bq1, bk1), more_params_loaded)
            for n, w in enumerate((wq, wk, wv, wo)):
                sp.dma_start(raw_qkvo[:, n], w.rearrange("(c p) n -> p c n", p=P)).then_inc(qkvo_loaded, 16)
            sp.dma_start(adj_a[:], adj_v[0]).then_inc(adj_a_loaded, 16)
            sp.dma_start(raw_2, w2.rearrange("(f p) n -> p f n", p=P)).then_inc(raw_2_loaded, 16)
            sp.dma_start(raw_1, w1.rearrange("(c p) n -> p c n", p=P)).then_inc(raw_1_loaded, 16)

            def prepare(i):
                if i == 0:
                    sp.wait_ge(hi_w, 2)
                    sp.wait_ge(lo_w, 2)
                    sp.wait_ge(prep_p, 4)
                    for n in range(LAYERS):
                        sp.dma_start(raw_l[:, n, 0], Wq[n]).then_inc(raw_l_loaded, 16)
                        sp.dma_start(raw_l[:, n, 1], Wk[n]).then_inc(raw_l_loaded, 16)
                        sp.dma_start(raw_l[:, n, 2:4], Wc[n].rearrange("(c p) d -> p c d", p=P))\
                            .then_inc(raw_l_loaded, 16)

            def body(i):
                if on(i - 2):
                    wait(sp, adj_l_used, i - 2)
                    sp.dma_start(adj_l[:], adj_v[i - 2]).then_inc(adj_l_loaded, 16)
                if on(i - 3):
                    wait(sp, l_out, i - 2)
                    sp.dma_start(out_v[i - 3], x3[:]).then_inc(stored, 16)
                if on(i + 1) and (not isinstance(i, int) or i >= 0):
                    wait(sp, x_used, i + 1)
                    sp.dma_start(x_in[:], x_v[i + 1]).then_inc(x_loaded, 16)
                    wait(sp, adj_a_used, i + 1)
                    sp.dma_start(adj_a[:], adj_v[i + 1]).then_inc(adj_a_loaded, 16)

            run(sp, body, prepare)
            sp.wait_ge(stored, 16 * GROUPS)

        @block.tensor
        def _(pe):
            def product(dst, lhs, rhs, terms):
                parts = ((0, 0), (1, 0), (0, 1))
                n = len(terms) * len(parts)
                k = 0
                for t in terms:
                    for a, b in parts:
                        last = nc.tensor.matmul(dst, lhs(t, a), rhs(t, b), start=(k == 0), stop=(k == n - 1))
                        k += 1
                return last

            def turn(ring, g, job, src, c):
                dst = wait_empty(pe, ring, g, job)
                for t in range(TILES):
                    last = nc.tensor.transpose(dst[:, t * P:(t + 1) * P], src[:, t, c * P:(c + 1) * P], ident[:])
                last.then_inc(is_filled(ring, job), 1)

            mm = nc.tensor.matmul

            def prepare(i):
                if i == -1:
                    pe.wait_ge(consts, 4)
                    n = PARAMS[0]
                    pe.wait_ge(params_loaded, 16 * PARAM_LOADS)
                    nc.tensor.transpose(bank[7][:, 0:n], param_rows[0], ident[0:n, 0:n]).then_inc(prep_p, 1)
                    n = PARAMS[1]
                    pe.wait_ge(more_params_loaded, 16 * PARAM_LOADS)
                    nc.tensor.transpose(bank[4][:, 0:n], param_rows[1], ident[0:n, 0:n]).then_inc(prep_p, 1)
                    pe.wait_ge(prep_d, 1)
                    pe.wait_ge(qkvo_loaded, 64)
                    for w in range(3):
                        for o in range(DC):
                            for c in range(DC):
                                last = mm(bank[6][:, 2 * w + o:2 * w + o + 1], raw_qkvo[:, w, c, o * P:(o + 1) * P],
                                          b1c[:, c:c + 1], start=(c == 0), stop=(c == DC - 1))
                    last.then_inc(prep_p, 1)
                    pe.wait_ge(prep_d, 3)
                    for c in range(DC):
                        last = mm(bank[5][:, 0:D], bv_c[:, c:c + 1].to_broadcast([P, P]), raw_qkvo[:, 3, c, :],
                                  start=(c == 0), stop=(c == DC - 1))
                    last.then_inc(prep_p, 1)
                if i == 0:
                    pe.wait_ge(hi_w, 1)
                    pe.wait_ge(lo_w, 1)
                if i == 1:
                    pe.wait_ge(prep_d, 6)
                    turn_w_c(1)

            def prepare_later():
                pe.wait_ge(prep_d, 4)
                pe.wait_ge(raw_1_loaded, 16)
                for f in range(FC):
                    for c in range(DC):
                        last = mm(bank[7][:, 32 + f:33 + f], raw_1[:, c, f * P:(f + 1) * P], b2c[:, c:c + 1],
                                  start=(c == 0), stop=(c == DC - 1))
                last.then_inc(prep_p, 1)
                pe.wait_ge(prep_d, 5)
                pe.wait_ge(raw_l_loaded, 96)
                for n in range(LAYERS):
                    for w in range(2):
                        for c in range(DC):
                            last = nc.tensor.transpose(bank[4 + n][:, (w * DC + c) * P:(w * DC + c + 1) * P],
                                                       raw_l[:, n, w, c * P:(c + 1) * P], ident[:])
                turn_w_c(0)

            def turn_w_c(n):
                for c in range(DC):
                    for e in range(DC):
                        last = nc.tensor.transpose(bank[6 + n][:, c * D + e * P:c * D + (e + 1) * P],
                                                   raw_l[:, n, 2 + e, c * P:(c + 1) * P], ident[:])
                last.then_inc(prep_p, 1)

            def a_turn(g):
                wait(pe, x_hat_ready, TILES * g + TILES)
                for c in range(DC):
                    turn("A", g, A_JOBS["xT"] + c, x_hat, c)

            def a_qk(g, w):
                for o in range(DC):
                    job = A_JOBS["qk"[w]] + o
                    dst = wait_sources(pe, "A", g, [A_JOBS["xT"], A_JOBS["xT"] + 1], job)
                    product(dst[:], lambda c, s: w_qkv[s][:, w, c, o * P:(o + 1) * P], lambda c, s: xT[s][:, c, :],
                            range(DC)).then_inc(is_filled("A", job), 1)

            def a_v(g):
                for k in range(2):
                    job = A_JOBS["v"] + k
                    dst = wait_empty(pe, "A", g, job)
                    for t in (2 * k, 2 * k + 1):
                        last = product(dst[:, t % 2 * D:(t % 2 + 1) * D], lambda c, s: xT[s][:, c, t * P:(t + 1) * P],
                                       lambda c, s: w_qkv[s][:, 2, c, :], range(DC))
                    last.then_inc(is_filled("A", job), 1)

            def a_scores(g, t):
                job = A_JOBS["s"] + t
                dst = wait_sources(pe, "A", g, range(A_JOBS["q"], A_JOBS["k"] + DC), job)
                for c in range(DC):
                    for b in range(2):
                        n = 2 * t + b
                        last = mm(dst[b * NODES:(b + 1) * NODES, c * 256:(c + 1) * 256],
                                  qT[:, c, n * NODES:(n + 1) * NODES],
                                  kT[:, c, n].rearrange("p j k -> p (j k)"), start=True, stop=True)
                last.then_inc(is_filled("A", job), 1)
                if isinstance(g, int) and g == 0 and t == TILES - 1:
                    prepare_later()

            def a_turn_p(g, t):
                wait(pe, p_ready, TILES * g + t + 1)
                job = P_JOB[t]
                dst = wait_empty(pe, "A", g, job)
                for j in range(H // 2):
                    last = nc.tensor.transpose(dst[:, j * P:(j + 1) * P], sc[:, t, j * P:(j + 1) * P], ident[:])
                last.then_inc(is_filled("A", job), 1)

            def a_values(g, k):
                job = O_JOB[k]
                dst = wait_sources(pe, "A", g, [A_JOBS["v"], A_JOBS["v"] + 1, P_JOB[2 * k], P_JOB[2 * k + 1]], job)
                for t in (2 * k, 2 * k + 1):
                    for b in range(2):
                        for j in range(H // 2):
                            at = (t % 2) * 256 + (j // 2) * P + b * NODES
                            last = mm(dst[j % 2 * 64:j % 2 * 64 + 64, at:at + NODES],
                                      v2[:, 2 * t + b, j].rearrange("p a d -> p (a d)"),
                                      pT[:, t % 2, j * P + b * NODES:j * P + (b + 1) * NODES], start=True, stop=True)
                last.then_inc(is_filled("A", job), 1)

            def a_out(g, k):
                if isinstance(g, int) and g == 0 and k == 0:
                    pe.wait_ge(hi_w, 2)
                    pe.wait_ge(lo_w, 2)
                job = A_JOBS["w"] + k
                dst = wait_sources(pe, "A", g, [O_JOB[k]], job)
                for t in (2 * k, 2 * k + 1):
                    last = product(dst[:, t % 2 * D:(t % 2 + 1) * D], lambda c, s: oT[s][:, c, t * P:(t + 1) * P],
                                   lambda c, s: w_o[s][:, c, :], range(DC))
                last.then_inc(is_filled("A", job), 1)

            def h_turn(g):
                if isinstance(g, int) and g == 0:
                    pe.wait_ge(hi_w, 8)
                    pe.wait_ge(lo_w, 8)
                wait(pe, x1_hat_ready, TILES * g + TILES)
                for c in range(DC):
                    turn("M", g, M_JOBS["xT"] + c, x1_hat, c)

            def h_up(g, f):
                job = M_JOBS["h"] + f
                dst = wait_sources(pe, "M", g, [M_JOBS["xT"], M_JOBS["xT"] + 1], job)
                product(dst[:], lambda c, s: w_1[s][:, c, f * P:(f + 1) * P], lambda c, s: nT[s][:, c, :],
                        range(DC)).then_inc(is_filled("M", job), 1)

            def y_down(g, t):
                job = M_JOBS["y"] + t // 2
                if t == 0:
                    wait(pe, h_lo, FC * g + FC)
                dst = wait_empty(pe, "M", g, job) if t % 2 == 0 else bank[BASE["M"] + job % RING["M"]]
                last = product(dst[:, t % 2 * D:(t % 2 + 1) * D], lambda f, s: hT[s][:, f, t * P:(t + 1) * P],
                               lambda f, s: w_2[s][:, f, :], range(FC))
                if t % 2:
                    last.then_inc(is_filled("M", job), 1)

            def l_turn(g, l):
                if l == 0:
                    for k in range(2):
                        wait_drained(pe, "M", g, M_JOBS["y"] + k)
                else:
                    wait(pe, l_x, TILES * g + TILES)
                for c in range(DC):
                    turn("L", g, L_JOBS[f"xT{l}"] + c, (x2, x3)[l], c)

            def l_qk(g, l):
                for w in range(2):
                    job = L_JOBS[f"qk{l}"] + w
                    dst = wait_sources(pe, "L", g, [L_JOBS[f"xT{l}"], L_JOBS[f"xT{l}"] + 1], job)
                    product(dst[:], lambda c, s: w_l[s][:, l, w, c, :], lambda c, s: lT[s][:, c, :],
                            range(DC)).then_inc(is_filled("L", job), 1)

            def l_xw(g, l):
                for k in range(2):
                    job = L_JOBS[f"xw{l}"] + k
                    dst = wait_empty(pe, "L", g, job)
                    for t in (2 * k, 2 * k + 1):
                        last = product(dst[:, t % 2 * D:(t % 2 + 1) * D], lambda c, s: lT[s][:, c, t * P:(t + 1) * P],
                                       lambda c, s: w_c[s][:, l, c, :], range(DC))
                    last.then_inc(is_filled("L", job), 1)

            def l_scores(g, l):
                job = L_JOBS[f"s{l}"]
                dst = wait_sources(pe, "L", g, [L_JOBS[f"qk{l}"], L_JOBS[f"qk{l}"] + 1], job)
                for t in range(TILES):
                    for b in range(2):
                        at = slice(t * P + b * NODES, t * P + (b + 1) * NODES)
                        last = mm(dst[b * NODES:(b + 1) * NODES, t * NODES:(t + 1) * NODES], lqk[:, 0, at],
                                  lqk[:, 1, at], start=True, stop=True)
                last.then_inc(is_filled("L", job), 1)

            def l_turn_p(g, l):
                job = L_JOBS[f"p{l}"]
                dst = wait_empty(pe, "L", g, job)
                wait(pe, l_exp, 2 * (2 * g + l + 1))
                for t in range(TILES):
                    last = nc.tensor.transpose(dst[:, t * P:(t + 1) * P], le[:, t], ident[:])
                last.then_inc(is_filled("L", job), 1)

            def l_mix(g, l):
                for k in range(2):
                    job = L_JOBS[f"o{l}"] + k
                    sources = [L_JOBS[f"p{l}"], L_JOBS[f"xw{l}"], L_JOBS[f"xw{l}"] + 1]
                    dst = wait_sources(pe, "L", g, sources, job)
                    for t in (2 * k, 2 * k + 1):
                        last = mm(dst[:, t % 2 * D:(t % 2 + 1) * D], lpT[:, t], lxw[:, t], start=True, stop=True)
                    last.then_inc(is_filled("L", job), 1)

            def body(i):
                if on(i - 3):
                    l_turn_p(i - 3, 1)
                if on(i):
                    a_turn(i)
                if on(i - 3):
                    l_mix(i - 3, 1)
                if on(i - 2):
                    y_down(i - 2, 1)
                if on(i):
                    a_qk(i, 0)
                if on(i - 2):
                    y_down(i - 2, 2)
                if on(i):
                    a_qk(i, 1)
                if on(i - 2):
                    y_down(i - 2, 3)
                if on(i):
                    a_v(i)
                if on(i - 1):
                    h_turn(i - 1)
                if on(i):
                    a_scores(i, 0)
                    a_scores(i, 1)
                if on(i - 2):
                    l_turn(i - 2, 0)
                if on(i):
                    a_scores(i, 2)
                    a_scores(i, 3)
                if on(i - 1):
                    h_up(i - 1, 0)
                    h_up(i - 1, 1)
                if on(i - 2):
                    l_qk(i - 2, 0)
                if on(i):
                    a_turn_p(i, 0)
                if on(i - 2):
                    l_xw(i - 2, 0)
                    l_scores(i - 2, 0)
                if on(i):
                    a_turn_p(i, 1)
                if on(i - 1):
                    h_up(i - 1, 2)
                    h_up(i - 1, 3)
                if on(i - 2):
                    l_turn_p(i - 2, 0)
                if on(i):
                    a_values(i, 0)
                if on(i - 2):
                    l_mix(i - 2, 0)
                if on(i):
                    a_turn_p(i, 2)
                if on(i - 1):
                    h_up(i - 1, 4)
                if on(i):
                    a_turn_p(i, 3)
                if on(i - 1):
                    h_up(i - 1, 5)
                if on(i):
                    a_values(i, 1)
                    a_out(i, 0)
                if on(i - 1):
                    h_up(i - 1, 6)
                    h_up(i - 1, 7)
                if on(i - 2):
                    l_turn(i - 2, 1)
                if on(i):
                    a_out(i, 1)
                if on(i - 2):
                    l_qk(i - 2, 1)
                    l_xw(i - 2, 1)
                    l_scores(i - 2, 1)
                if on(i - 1):
                    y_down(i - 1, 0)

            run(pe, body, prepare)

        @block.scalar
        def _(act):
            def prepare(i):
                if i == 0:
                    act.wait_ge(prep_d, 1)
                    act.wait_ge(qkvo_loaded, 64)
                    for c in range(DC):
                        last = nc.scalar.activation(w_qkv[0][:, :, c], raw_qkvo[:, 0:3, c], ACT.Identity,
                                                    scale=g1c[:, c:c + 1])
                    last.then_inc(hi_w, 1)
                    nc.scalar.activation(w_o[0][:], raw_qkvo[:, 3], ACT.Identity).then_inc(hi_w, 1)
                    act.wait_ge(raw_2_loaded, 16)
                    nc.scalar.activation(w_2[0][:], raw_2, ACT.Identity).then_inc(hi_w, 1)
                    act.wait_ge(prep_d, 4)
                    act.wait_ge(raw_1_loaded, 16)
                    for c in range(DC):
                        last = nc.scalar.activation(w_1[0][:, c], raw_1[:, c], ACT.Identity, scale=g2c[:, c:c + 1])
                    last.then_inc(hi_w, 1)
                    act.wait_ge(zeroed, 2)
                if i == 1:
                    for n in range(LAYERS):
                        act.wait_ge(prep_p, 6 + n)
                        for turned, hi, _ in turned_weights(n):
                            nc.scalar.activation(hi, turned, ACT.Identity).then_inc(hi_w, 1)

            def a_hi(g):
                for c in range(DC):
                    src = wait_filled(act, "A", g, A_JOBS["xT"] + c)
                    nc.scalar.activation(xT[0][:, c], src[:], ACT.Identity).then_inc(hi_a, 1)

            def a_qk(g):
                for c in range(DC):
                    job = A_JOBS["q"] + c
                    src = wait_filled(act, "A", g, job)
                    nc.scalar.activation(qT[:, c], src[:], ACT.Identity, bias=bq_c[:, c:c + 1],
                                         scale=SCALE0).then_inc(is_drained("A", job), 1)
                for c in range(DC):
                    job = A_JOBS["k"] + c
                    src = wait_filled(act, "A", g, job)
                    for j in range(QUADS):
                        at = slice(j * HD, (j + 1) * HD)
                        last = nc.scalar.activation(kT[at, c, :, j, :], src[at, :].rearrange("p (g k) -> p g k", k=NODES),
                                                    ACT.Identity, bias=bk_c[at, c:c + 1])
                    last.then_inc(is_drained("A", job), 1)

            def a_v(g):
                for k in range(2):
                    job = A_JOBS["v"] + k
                    src = wait_filled(act, "A", g, job)[:].rearrange("p (t j a d) -> p t j a d", t=2, a=2, d=HD)
                    for b in range(2):
                        for a in range(2):
                            dst = v2[a * 64:(a + 1) * 64].rearrange("p (t b) j a d -> p t b j a d", b=2)
                            last = nc.scalar.activation(dst[:, 2 * k:2 * k + 2, b, :, a, :],
                                                        src[b * 64:(b + 1) * 64, :, :, a, :], ACT.Identity)
                    last.then_inc(is_drained("A", job), 1)

            def a_exp(g, t):
                wait(act, shifted, TILES * g + t + 1)
                nc.scalar.activation(sc[:, t], sc[:, t], ACT.Exp).then_inc(exp_done, 1)

            def a_copy_p(g, t):
                src = wait_filled(act, "A", g, P_JOB[t])
                nc.scalar.activation(pT[:, t % 2], src[:], ACT.Identity).then_inc(is_drained("A", P_JOB[t]), 1)

            def a_hi_o(g, k):
                src = wait_filled(act, "A", g, O_JOB[k])[:].rearrange("p (t c r) -> p t c r", t=2, c=DC)
                dst = oT[0][:].rearrange("p c (t r) -> p t c r", r=P)[:, 2 * k:2 * k + 2]
                nc.scalar.activation(dst, src, ACT.Identity).then_inc(hi_a, 1)

            def h_hi_x(g):
                for c in range(DC):
                    src = wait_filled(act, "M", g, M_JOBS["xT"] + c)
                    nc.scalar.activation(nT[0][:, c], src[:], ACT.Identity).then_inc(hi_m, 1)

            def h_gelu(g, f):
                if isinstance(g, int) and g == 0 and f == 0:
                    act.wait_ge(prep_d, 6)
                    act.wait_ge(lo_w, 8)
                wait(act, h_lo, FC * g + max(f - HB + 1, 0))
                job = M_JOBS["h"] + f
                src = wait_filled(act, "M", g, job)
                nc.scalar.activation(hf[:, f % HB], src[:], ACT.Gelu, bias=bh_c[:, f:f + 1])
                nc.scalar.activation(hT[0][:, f], src[:], ACT.Gelu, bias=bh_c[:, f:f + 1])\
                    .then_inc(is_drained("M", job), 1)

            def l_hi(g, l):
                for c in range(DC):
                    src = wait_filled(act, "L", g, L_JOBS[f"xT{l}"] + c)
                    nc.scalar.activation(lT[0][:, c], src[:], ACT.Identity).then_inc(hi_l, 1)

            def l_copies(g, l):
                for w in range(2):
                    job = L_JOBS[f"qk{l}"] + w
                    src = wait_filled(act, "L", g, job)
                    nc.scalar.activation(lqk[:, w], src[:], ACT.Identity, bias=(lq_c, lk_c)[w][:, l:l + 1],
                                         scale=(SCALE1, 1.0)[w]).then_inc(is_drained("L", job), 1)
                for k in range(2):
                    job = L_JOBS[f"xw{l}"] + k
                    src = wait_filled(act, "L", g, job)
                    nc.scalar.activation(lxw[:, 2 * k:2 * k + 2].rearrange("p t d -> p (t d)"), src[:], ACT.Identity)\
                        .then_inc(is_drained("L", job), 1)

            def l_exps(g, l):
                wait(act, l_top, 2 * g + l + 1)
                for b in range(2):
                    at = slice(b * NODES, (b + 1) * NODES)
                    nc.scalar.activation(le[at, :, at], ls[at], ACT.Exp).then_inc(l_exp, 1)

            def l_copy_p(g, l):
                job = L_JOBS[f"p{l}"]
                src = wait_filled(act, "L", g, job)
                nc.scalar.activation(lqk[:, 0, :], src[:], ACT.Identity)\
                    .then_inc(is_drained("L", job), 1)

            def body(i):
                if on(i):
                    a_hi(i)
                    a_qk(i)
                if on(i - 1):
                    h_hi_x(i - 1)
                if on(i):
                    a_v(i)
                    a_exp(i, 0)
                if on(i - 2):
                    l_hi(i - 2, 0)
                if on(i):
                    a_exp(i, 1)
                if on(i - 1):
                    h_gelu(i - 1, 0)
                    h_gelu(i - 1, 1)
                if on(i - 2):
                    l_copies(i - 2, 0)
                if on(i):
                    a_exp(i, 2)
                    a_copy_p(i, 0)
                if on(i - 2):
                    l_exps(i - 2, 0)
                if on(i):
                    a_copy_p(i, 1)
                    a_exp(i, 3)
                if on(i - 2):
                    l_copy_p(i - 2, 0)
                if on(i - 1):
                    h_gelu(i - 1, 2)
                if on(i):
                    a_hi_o(i, 0)
                if on(i - 1):
                    h_gelu(i - 1, 3)
                if on(i):
                    a_copy_p(i, 2)
                    a_copy_p(i, 3)
                if on(i - 1):
                    h_gelu(i - 1, 4)
                if on(i):
                    a_hi_o(i, 1)
                if on(i - 1):
                    h_gelu(i - 1, 5)
                if on(i - 2):
                    l_hi(i - 2, 1)
                if on(i - 1):
                    h_gelu(i - 1, 6)
                    h_gelu(i - 1, 7)
                if on(i - 2):
                    l_copies(i - 2, 1)
                    l_exps(i - 2, 1)
                    l_copy_p(i - 2, 1)

            run(act, body, prepare)

        @block.gpsimd
        def _(pool):
            nc.gpsimd.memset(ident[:], 0.0).then_inc(consts, 1)
            nc.gpsimd.memset(minus_half, -0.5).then_inc(consts, 1)
            nc.gpsimd.memset(le[:], 0.0).then_inc(consts, 1)
            pool.wait_ge(consts, 3)
            nc.gpsimd.affine_select(out=ident[:], in_=ident[:], compare_op=ALU.not_equal, fill=1.0, base=0,
                                    pattern=[[-1, P]], channel_multiplier=1).then_inc(consts, 1)
            row = lambda v: v.rearrange("(a n) -> a n", a=1).to_broadcast([P, v.shape[0]])
            pool.dma_start(bo_row[:], row(bo)).then_inc(bo_loaded, 16)

            def prepare(i):
                if i == 0:
                    nc.gpsimd.memset(kT[:], 0.0).then_inc(zeroed, 1)
                    nc.gpsimd.memset(v2[:], 0.0).then_inc(zeroed, 1)
                    pool.dma_start(b2_row[:], row(b2)).then_inc(rows_loaded, 16)
                    for n in range(LAYERS):
                        pool.dma_start(lg_row[:, n], row(ln_g[n])).then_inc(rows_loaded, 16)
                        pool.dma_start(lb_row[:, n], row(ln_b[n])).then_inc(rows_loaded, 16)

            def normalise(g, s, src, dst, chain, ready):
                _, _, nm, ve, rs = stats[s]
                wait(pool, {"A": stats_a, "H": stats_h}[s], 2 * g + 2)
                nc.gpsimd.tensor_tensor(rs[:], ve[:], minus_half, ALU.pow).then_inc(chain, 1)
                wait(pool, chain, g + 1)
                nc.gpsimd.tensor_tensor(spare_p, minus_half[:, 0:1], minus_half[:, 0:1], ALU.add)
                for t in range(TILES):
                    nc.gpsimd.tensor_scalar(dst[:, t], src[:, t], nm[:, t:t + 1], rs[:, t:t + 1], ALU.add,
                                            ALU.mult).then_inc(ready, 1)

            def a_normalise(g):
                normalise(g, "A", x_in, x_hat, pool_a, x_hat_ready)

            def a_add_bo(g):
                if isinstance(g, int) and g == 0:
                    pool.wait_ge(prep_d, 5)
                wait(pool, x1_b2_ready, g)
                wait(pool, x1_hat_ready, TILES * g)
                nc.gpsimd.tensor_tensor(x1[:], x_in[:], bo_row[:].rearrange("p (t d) -> p t d", t=1)
                                        .to_broadcast([P, TILES, D]), ALU.add).then_inc(x1_begun, 1)
                wait(pool, x1_begun, g + 1)
                pool.sem_inc(x_used, 1)

            def h_normalise(g):
                if on(g + 1):
                    for c in range(DC):
                        wait_filled(pool, "A", g + 1, A_JOBS["xT"] + c)
                normalise(g, "H", x1, x1_hat, pool_h, x1_hat_ready)

            def h_add_b2(g):
                if isinstance(g, int) and g == 0:
                    pool.wait_ge(rows_loaded, 16 * ROW_LOADS)
                    pool.wait_ge(lo_w, 8)
                for k in range(2):
                    wait_drained_before(pool, "M", g, M_JOBS["y"] + k)
                nc.gpsimd.tensor_tensor(x1_b2[:], x1[:], b2_row[:].rearrange("p (t d) -> p t d", t=1)
                                        .to_broadcast([P, TILES, D]), ALU.add).then_inc(x1_b2_ready, 1)

            def l_rstd(g, l):
                _, _, nm, ve, rs = stats["L"]
                wait(pool, stats_l, 2 * (2 * g + l + 1))
                nc.gpsimd.tensor_tensor(rs[:], ve[:], minus_half, ALU.pow).then_inc(rstd_l, 1)

            def body(i):
                if on(i - 3):
                    l_rstd(i - 3, 1)
                if on(i - 1):
                    h_normalise(i - 1)
                    h_add_b2(i - 1)
                if on(i):
                    a_add_bo(i)
                if on(i - 2):
                    l_rstd(i - 2, 0)
                if on(i + 1):
                    a_normalise(i + 1)

            run(pool, body, prepare)

        @block.vector
        def _(dve):
            tt = nc.vector.tensor_tensor
            ts = nc.vector.tensor_scalar
            stt = nc.vector.scalar_tensor_tensor

            def prepare(i):
                if i == -1:
                    n, m = PARAMS
                    dve.wait_ge(prep_p, 1)
                    nc.vector.tensor_copy(cols[:, 0:n], bank[7][:, 0:n]).then_inc(prep_d, 1)
                if i == 0:
                    n, m = PARAMS
                    dve.wait_ge(prep_p, 2)
                    nc.vector.tensor_copy(cols[:, n:n + m], bank[4][:, 0:m]).then_inc(prep_d, 1)
                    dve.wait_ge(prep_p, 3)
                    tt(cols[:, 4:10], cols[:, 4:10], bank[6][:, 0:6], ALU.add).then_inc(prep_d, 1)
                    dve.wait_ge(prep_d, 3)
                    ts(bq_c, bq_c, SCALE0, None, ALU.mult).then_inc(prep_d, 1)
                    dve.wait_ge(hi_w, 1)
                    for c in range(DC):
                        last = stt(w_qkv[1][:, :, c], raw_qkvo[:, 0:3, c], g1c[:, c:c + 1],
                                   w_qkv[0][:, :, c].bitcast(F32), ALU.mult, ALU.subtract)
                    last.then_inc(lo_w, 1)
                    dve.wait_ge(hi_w, 2)
                    tt(w_o[1][:], raw_qkvo[:, 3], w_o[0][:].bitcast(F32), ALU.subtract).then_inc(lo_w, 1)
                    dve.wait_ge(bo_loaded, 16)
                    dve.wait_ge(prep_p, 4)
                    tt(bo_row[:], bo_row[:], bank[5][:, 0:D], ALU.add).then_inc(prep_d, 1)
                if i == 1:
                    dve.wait_ge(prep_p, 5)
                    tt(bh_c, bh_c, bank[7][:, 32:40], ALU.add)
                    ts(lq_c, lq_c, SCALE1, None, ALU.mult).then_inc(prep_d, 1)
                    for n in range(LAYERS):
                        for k, (turned, hi, lo) in enumerate(turned_weights(n)):
                            dve.wait_ge(hi_w, 5 + 2 * n + k)
                            tt(lo, turned, hi.bitcast(F32), ALU.subtract).then_inc(lo_w, 1)
                    dve.wait_ge(rows_loaded, 16 * ROW_LOADS)

            def prepare_mlp():
                dve.wait_ge(hi_w, 3)
                tt(w_2[1][:], raw_2, w_2[0][:].bitcast(F32), ALU.subtract).then_inc(lo_w, 1)
                dve.wait_ge(hi_w, 4)
                dve.wait_ge(prep_d, 4)
                for c in range(DC):
                    last = stt(w_1[1][:, c], raw_1[:, c], g2c[:, c:c + 1], w_1[0][:, c].bitcast(F32), ALU.mult,
                               ALU.subtract)
                last.then_inc(lo_w, 1)

            class Chain:

                def __init__(self, s, per_group, g, n=0):
                    self.s, self.base, self.n = s, g * per_group, n

                def step(self, ins):
                    self.n += 1
                    ins.then_inc(self.s, 1)

                def wait(self):
                    wait(dve, self.s, self.base + self.n)

            def norm_stats(s, src, chain, ready):
                st, mv, nm, ve, rs = stats[s]
                for t in range(TILES):
                    ins = nc.vector.bn_stats(st[:, t], src[:, t])
                chain.step(ins)
                chain.wait()
                nc.vector.memset(spare_d, 0.0)
                for t in range(TILES):
                    ins = nc.vector.bn_aggr(mv[:, t], st[:, t])
                chain.step(ins)
                chain.wait()
                ts(nm[:], mv[:, :, 0], -1.0, None, ALU.mult).then_inc(ready, 1)
                ts(ve[:], mv[:, :, 1], EPS, None, ALU.add).then_inc(ready, 1)

            N_STEPS = 2
            A_STEPS = 1 + 3 * TILES
            H_STEPS = 2
            L_STEPS = LAYERS * 6

            def a_norm(g, ch):
                wait(dve, x_loaded, 16 * g + 16)
                norm_stats("A", x_in, ch, stats_a)

            def a_edges(g, ch):
                wait(dve, adj_a_loaded, 16 * g + 16)
                stt(bias0[:], adj_a[:], 0.1, adj_a[:], ALU.mult, ALU.mult)
                ts(pen[:], adj_a[:], 0, MASKED, ALU.is_le, ALU.mult).then_inc(adj_a_used, 1)
                wait(dve, adj_a_used, g + 1)
                ch.step(tt(bias0[:], bias0[:], pen[:], ALU.add))
                if isinstance(g, int) and g == 0:
                    prepare_mlp()

            def lo_of(ring, g, job, hi_sem, count, hi, lo, view=None):
                src = wait_filled(dve, ring, g, job)[:]
                if view:
                    src = view(src)
                wait(dve, hi_sem, count)
                tt(lo, src, hi.bitcast(F32), ALU.subtract).then_inc(is_drained(ring, job), 1)

            def a_lo(g):
                for c in range(DC):
                    lo_of("A", g, A_JOBS["xT"] + c, hi_a, 4 * g + c + 1, xT[0][:, c], xT[1][:, c])

            heads = lambda a: a.rearrange("p (h k) -> p h k", h=H)
            spread = lambda a: a.rearrange("p (h k) -> p h k", k=1).to_broadcast([P, H, NODES])

            def a_front(g, t, ch):
                job = A_JOBS["s"] + t
                src = wait_filled(dve, "A", g, job)
                s = heads(sc[:, t])
                if t == 0:
                    ch.wait()
                tt(s, heads(src[:]), bias0[:, t].rearrange("p (h k) -> p h k", h=1).to_broadcast([P, H, NODES]),
                   ALU.add).then_inc(is_drained("A", job), 1)
                wait_drained(dve, "A", g, job)
                ch.step(nc.vector.reduce_max(top[:, t], s, AX_X))
                ch.wait()
                tt(s, s, spread(top[:, t]), ALU.subtract).then_inc(shifted, 1)

            def a_back(g, t, ch):
                wait(dve, exp_done, TILES * g + t + 1)
                e = heads(sc[:, t])
                ch.step(nc.vector.reduce_sum(total[:, t], e, AX_X))
                ch.wait()
                ch.step(nc.vector.reciprocal(share[:, t], total[:, t]))
                ch.wait()
                tt(heads(sc[:, t]), e, spread(share[:, t]), ALU.mult).then_inc(p_ready, 1)

            def a_lo_o(g, k):
                dst = [oT[s][:].rearrange("p c (t r) -> p t c r", r=P)[:, 2 * k:2 * k + 2] for s in range(2)]
                lo_of("A", g, O_JOB[k], hi_a, 4 * g + 3 + k, dst[0], dst[1],
                      lambda b: b.rearrange("p (t c r) -> p t c r", t=2, c=DC))

            def a_residual(g, k):
                wait(dve, x1_begun, g + 1)
                job = A_JOBS["w"] + k
                src = wait_filled(dve, "A", g, job)
                tt(x1[:, 2 * k:2 * k + 2], src[:].rearrange("p (t d) -> p t d", t=2), x1[:, 2 * k:2 * k + 2],
                   ALU.add).then_inc(is_drained("A", job), 1)

            def h_norm(g, ch):
                for k in range(2):
                    wait_drained(dve, "A", g, A_JOBS["w"] + k)
                norm_stats("H", x1, ch, stats_h)

            def h_lo_x(g):
                for c in range(DC):
                    lo_of("M", g, M_JOBS["xT"] + c, hi_m, DC * g + c + 1, nT[0][:, c], nT[1][:, c])

            def h_rest(g, f):
                wait_drained(dve, "M", g, M_JOBS["h"] + f)
                tt(hT[1][:, f], hf[:, f % HB], hT[0][:, f].bitcast(F32), ALU.subtract).then_inc(h_lo, 1)

            def y_residual(g, k):
                wait(dve, x1_b2_ready, g + 1)
                job = M_JOBS["y"] + k
                src = wait_filled(dve, "M", g, job)
                tt(x2[:, 2 * k:2 * k + 2], src[:].rearrange("p (t d) -> p t d", t=2), x1_b2[:, 2 * k:2 * k + 2],
                   ALU.add).then_inc(is_drained("M", job), 1)

            def l_mask(g):
                wait(dve, adj_l_loaded, 16 * g + 16)
                ts(pen1[:], adj_l[:], 0, MASKED, ALU.is_equal, ALU.mult).then_inc(adj_l_used, 1)
                wait(dve, adj_l_used, g + 1)

            def l_lo(g, l):
                for c in range(DC):
                    lo_of("L", g, L_JOBS[f"xT{l}"] + c, hi_l, 2 * DC * g + DC * l + c + 1, lT[0][:, c], lT[1][:, c])

            def l_front(g, l, ch):
                job = L_JOBS[f"s{l}"]
                src = wait_filled(dve, "L", g, job)
                tt(ls[:], src[:, 0:TILES * NODES].rearrange("p (t n) -> p t n", t=TILES), pen1[:], ALU.add)\
                    .then_inc(is_drained("L", job), 1)
                wait_drained(dve, "L", g, job)
                ch.step(nc.vector.reduce_max(ltop[:], ls[:], AX_X))
                ch.wait()
                tt(ls[:], ls[:], ltop[:].rearrange("p (t n) -> p t n", n=1).to_broadcast([P, TILES, NODES]),
                   ALU.subtract).then_inc(l_top, 1)

            def l_mix(g, l, ch):
                wait(dve, l_exp, 2 * (2 * g + l + 1))
                ch.step(nc.vector.reduce_sum(lsum[:], le[:], AX_X))
                ch.wait()
                ch.step(nc.vector.reciprocal(lshare[:], lsum[:]))
                ch.wait()
                prev = (x2, x3)[l]
                if l == 0:
                    for k in range(2):
                        wait_drained(dve, "M", g, M_JOBS["y"] + k)
                for t in range(TILES):
                    job = L_JOBS[f"o{l}"] + t // 2
                    src = wait_filled(dve, "L", g, job) if t % 2 == 0 else src
                    ins = stt(prev[:, t], src[:, t % 2 * D:(t % 2 + 1) * D], lshare[:, t:t + 1], prev[:, t], ALU.mult,
                              ALU.add)
                    if t % 2:
                        ins.then_inc(is_drained("L", job), 1)
                for k in range(2):
                    wait_drained(dve, "L", g, L_JOBS[f"o{l}"] + k)
                norm_stats("L", prev, ch, stats_l)

            def l_norm(g, l, ch):
                prev = (x2, x3)[l]
                _, _, nm, ve, rs = stats["L"]
                wait(dve, stats_l, 2 * (2 * g + l + 1))
                for t in range(TILES):
                    ins = stt(prev[:, t], prev[:, t], nm[:, t:t + 1], lg_row[:, l], ALU.add, ALU.mult)
                ch.step(ins)
                wait(dve, rstd_l, 2 * g + l + 1)
                ch.wait()
                if l == 0:
                    wait(dve, stored, 16 * g)
                for t in range(TILES):
                    ins = stt(x3[:, t], prev[:, t], rs[:, t:t + 1], lb_row[:, l], ALU.mult, ALU.add)
                    if l == 0:
                        ins.then_inc(l_x, 1)
                if l == 1:
                    ins.then_inc(l_out, 1)
                else:
                    wait(dve, l_x, TILES * g + TILES)

            def body(i):
                ca = Chain(dve_a, A_STEPS, i)
                cn = Chain(dve_n, N_STEPS, i + 1)
                ch = Chain(dve_h, H_STEPS, i - 1)
                cl = Chain(dve_l, L_STEPS, i - 2)
                ct = Chain(dve_l, L_STEPS, i - 3, L_STEPS // 2 + 1)
                if on(i):
                    a_lo(i)
                if on(i - 1):
                    h_norm(i - 1, ch)
                if on(i - 2):
                    l_mask(i - 2)
                if on(i - 3):
                    l_mix(i - 3, 1, ct)
                if on(i - 2):
                    y_residual(i - 2, 0)
                if on(i - 3):
                    l_norm(i - 3, 1, ct)
                if on(i - 2):
                    y_residual(i - 2, 1)
                if on(i):
                    a_edges(i, ca)
                if on(i - 1):
                    h_lo_x(i - 1)
                if on(i):
                    a_front(i, 0, ca)
                    a_front(i, 1, ca)
                if on(i - 2):
                    l_lo(i - 2, 0)
                if on(i):
                    a_back(i, 0, ca)
                    a_back(i, 1, ca)
                    a_front(i, 2, ca)
                    a_front(i, 3, ca)
                if on(i - 2):
                    l_front(i - 2, 0, cl)
                if on(i - 1):
                    h_rest(i - 1, 0)
                if on(i):
                    a_back(i, 2, ca)
                if on(i - 1):
                    h_rest(i - 1, 1)
                if on(i):
                    a_back(i, 3, ca)
                if on(i - 2):
                    l_mix(i - 2, 0, cl)
                if on(i - 1):
                    h_rest(i - 1, 2)
                if on(i):
                    a_lo_o(i, 0)
                if on(i - 1):
                    h_rest(i - 1, 3)
                if on(i - 2):
                    l_norm(i - 2, 0, cl)
                if on(i - 1):
                    h_rest(i - 1, 4)
                if on(i):
                    a_lo_o(i, 1)
                if on(i - 2):
                    l_lo(i - 2, 1)
                if on(i - 1):
                    h_rest(i - 1, 5)
                if on(i + 1):
                    a_norm(i + 1, cn)
                if on(i - 1):
                    h_rest(i - 1, 6)
                    h_rest(i - 1, 7)
                if on(i):
                    a_residual(i, 1)
                if on(i - 2):
                    l_front(i - 2, 1, cl)
                if on(i):
                    a_residual(i, 0)
                assert not on(i) or ca.n == A_STEPS
                assert not on(i + 1) or cn.n == N_STEPS
                assert not on(i - 1) or ch.n == H_STEPS
                assert not on(i - 2) or cl.n == L_STEPS // 2 + 1
                assert not on(i - 3) or ct.n == L_STEPS

            run(dve, body, prepare)


_INS = ['x', 'adj', 'L0_gnn_ln1_g', 'L0_gnn_ln1_b', 'L0_gnn_ln2_g', 'L0_gnn_ln2_b', 'L0_gnn_wq', 'L0_gnn_bq',
        'L0_gnn_wk', 'L0_gnn_bk', 'L0_gnn_wv', 'L0_gnn_bv', 'L0_gnn_wo', 'L0_gnn_bo', 'L0_gnn_w1', 'L0_gnn_b1',
        'L0_gnn_w2', 'L0_gnn_b2', 'L1_gnn_Wq', 'L1_gnn_bq', 'L1_gnn_Wk', 'L1_gnn_bk', 'L1_gnn_Wc', 'L1_gnn_ln_g',
        'L1_gnn_ln_b']


def kernel(**inputs):
    import numpy as _np
    import concourse.bacc as _bacc
    from concourse import mybir as _mybir
    from concourse.bass_utils import run_bass_kernel_spmd as _run

    nc = _bacc.Bacc("TRN2", target_bir_lowering=False, num_devices=1)
    arrays, args = {}, []
    for name in _INS:
        a = _np.ascontiguousarray(inputs[name])
        arrays[f"in_{name}_dram"] = a
        args.append(nc.dram_tensor(f"in_{name}_dram", a.shape, _mybir.dt.from_np(a.dtype), kind="ExternalInput").ap())
    shape = arrays["in_x_dram"].shape
    args.append(nc.dram_tensor("out_0_dram", shape, _mybir.dt.float32, kind="ExternalOutput").ap())
    gnn_kernel(nc, *args)
    r = _run(nc, [arrays], core_ids=[0])
    return r.results[0]["out_0_dram"]
```
